# Optimizing a Trainium2 kernel written in Bass

```python
import numpy as np
import jax
import jax.numpy as jnp

def _softmax(x, axis=-1):
    return jax.nn.softmax(x, axis=axis)

def _gelu(x):
    return jax.nn.gelu(x, approximate=True)

def _silu(x):
    return jax.nn.silu(x)

def _sigmoid(x):
    return jax.nn.sigmoid(x)

def _layernorm(x, axis=-1, eps=1e-05):
    m = jnp.mean(x, axis=axis, keepdims=True)
    v = jnp.var(x, axis=axis, keepdims=True)
    return (x - m) / jnp.sqrt(v + eps)

def _scatter_add(tgt, idx, src, axis=0):
    return tgt.at[idx].add(src)

def _segment_sum(src, seg, n):
    return jax.ops.segment_sum(src, seg, n)
kernel_name = 'mk_seq_postln_d1_jaxref_r8_450cb3'

def setup_inputs(seed: int=0):
    np.random.seed(seed)
    _w = jnp.asarray

    def _L0_attn_setup():
        import jax, jax.numpy as jnp
        import numpy as np
        import math
        EMBED_DIM = 128
        NUM_HEADS = 16
        HEAD_DIM = EMBED_DIM // NUM_HEADS
        key = jax.random.key(seed)
        ks = jax.random.split(key, 5)
        B, S, D = (2, 256, EMBED_DIM)
        s = 1.0 / math.sqrt(D)
        x = jax.random.normal(ks[0], (B, S, D), dtype=jnp.float32)
        W_qkv = jax.random.normal(ks[1], (3 * D, D), dtype=jnp.float32) * s
        b_qkv = jax.random.normal(ks[2], (3 * D,), dtype=jnp.float32) * 0.01
        W_out = jax.random.normal(ks[3], (D, D), dtype=jnp.float32) * s
        b_out = jax.random.normal(ks[4], (D,), dtype=jnp.float32) * 0.01
        return {'x': x, 'W_qkv': W_qkv, 'b_qkv': b_qkv, 'W_out': W_out, 'b_out': b_out}
    _L0_attn_in = _L0_attn_setup()

    def _L0_ffn_setup():
        import jax, jax.numpy as jnp
        import numpy as np
        TOP_K = 8
        key = jax.random.key(seed)
        ks = jax.random.split(key, 6)
        B, S, D, F, E = (2, 128, 128, 64, 64)
        x = jax.random.normal(ks[0], (B, S, D), dtype=jnp.float32)
        centroids = jax.random.normal(ks[1], (E, D), dtype=jnp.float32) * 0.05
        expert_biases = jnp.zeros((E,), dtype=jnp.float32)
        Ws_up = jax.random.normal(ks[2], (D, F), dtype=jnp.float32) / np.sqrt(D)
        Ws_down = jax.random.normal(ks[3], (F, D), dtype=jnp.float32) / np.sqrt(F)
        W_up = jax.random.normal(ks[4], (E, D, F), dtype=jnp.float32) / np.sqrt(D)
        W_down = jax.random.normal(ks[5], (E, F, D), dtype=jnp.float32) / np.sqrt(F)
        return {'x': x, 'centroids': centroids, 'expert_biases': expert_biases, 'Ws_up': Ws_up, 'Ws_down': Ws_down, 'W_up': W_up, 'W_down': W_down}
    _L0_ffn_in = _L0_ffn_setup()
    _d = {'L0_attn_x': _L0_attn_in['x'], 'L0_attn_W_qkv': _L0_attn_in['W_qkv'], 'L0_attn_b_qkv': _L0_attn_in['b_qkv'], 'L0_attn_W_out': _L0_attn_in['W_out'], 'L0_attn_b_out': _L0_attn_in['b_out'], 'L0_ffn_centroids': _L0_ffn_in['centroids'], 'L0_ffn_expert_biases': _L0_ffn_in['expert_biases'], 'L0_ffn_Ws_up': _L0_ffn_in['Ws_up'], 'L0_ffn_Ws_down': _L0_ffn_in['Ws_down'], 'L0_ffn_W_up': _L0_ffn_in['W_up'], 'L0_ffn_W_down': _L0_ffn_in['W_down']}
    _x0 = _d['L0_attn_x']
    _d['L0_attn_x'] = jax.random.normal(jax.random.fold_in(jax.random.key(seed), 1), (4, 1024, 128), dtype=_x0.dtype)
    del _x0
    return _d

def reference(L0_attn_x, L0_attn_W_qkv, L0_attn_b_qkv, L0_attn_W_out, L0_attn_b_out, L0_ffn_centroids, L0_ffn_expert_biases, L0_ffn_Ws_up, L0_ffn_Ws_down, L0_ffn_W_up, L0_ffn_W_down):

    def _L0_attn_ref(x, W_qkv, b_qkv, W_out, b_out):
        import jax, jax.numpy as jnp
        import numpy as np
        import math
        EMBED_DIM = 128
        NUM_HEADS = 16
        HEAD_DIM = EMBED_DIM // NUM_HEADS
        B, S, D = x.shape
        H, Hd = (NUM_HEADS, HEAD_DIM)
        slopes = jnp.power(2.0, 8.0 * jnp.arange(0, -H, -1, dtype=jnp.float32) / H)
        qkv = x @ W_qkv.T + b_qkv
        qkv = qkv.reshape(B, S, 3, H, Hd).transpose(2, 0, 3, 1, 4)
        q, k, v = (qkv[0], qkv[1], qkv[2])
        scores = jnp.einsum('bhqd,bhkd->bhqk', q, k) / math.sqrt(Hd)
        pos = jnp.arange(S)
        rel = jnp.abs(pos[None, :] - pos[:, None]).astype(jnp.float32)
        bias = -slopes[:, None, None] * rel
        probs = jax.nn.softmax(scores + bias[None], axis=-1)
        out = jnp.einsum('bhqk,bhkd->bhqd', probs, v)
        out = out.transpose(0, 2, 1, 3).reshape(B, S, D)
        return out @ W_out.T + b_out

    def _L0_ffn_ref(x, centroids, expert_biases, Ws_up, Ws_down, W_up, W_down):
        import jax, jax.numpy as jnp
        import numpy as np
        TOP_K = 8
        B, S, D = x.shape
        E = centroids.shape[0]
        T = B * S
        xf = x.reshape(T, D)
        shared = jax.nn.silu(xf @ Ws_up) @ Ws_down
        aff = xf @ centroids.T
        biased = aff + expert_biases
        _, idx = jax.lax.top_k(biased, TOP_K)
        sel = jnp.take_along_axis(aff, idx, axis=1)
        w = jax.nn.sigmoid(sel)
        w = w / (jnp.sum(w, axis=-1, keepdims=True) + 1e-08)
        cw = jnp.zeros((T, E), dtype=x.dtype).at[jnp.arange(T)[:, None], idx].add(w)
        h = jax.nn.silu(jnp.einsum('td,edf->etf', xf, W_up))
        y = jnp.einsum('etf,efd->etd', h, W_down)
        routed = jnp.einsum('etd,te->td', y, cw)
        return (shared + routed).reshape(B, S, D)
    x = L0_attn_x
    x = _layernorm(x + _L0_attn_ref(x, L0_attn_W_qkv, L0_attn_b_qkv, L0_attn_W_out, L0_attn_b_out), axis=-1)
    x = _layernorm(x + _L0_ffn_ref(x, L0_ffn_centroids, L0_ffn_expert_biases, L0_ffn_Ws_up, L0_ffn_Ws_down, L0_ffn_W_up, L0_ffn_W_down), axis=-1)
    return x

_drawn_inputs = setup_inputs


def setup_inputs(seed=0):
    import zlib

    import numpy as np

    out = dict(_drawn_inputs(seed))
    spreads = {'L0_ffn_expert_biases': (0.0, 0.1)}
    factors = {}
    for name, (base, spread) in spreads.items():
        noise = np.random.default_rng([zlib.crc32(name.encode()), seed]).standard_normal(out[name].shape)
        drawn = base * np.exp(spread * noise) if base else spread * noise
        out[name] = jnp.asarray(drawn.astype(out[name].dtype))
    for name, factor in factors.items():
        out[name] = (out[name] * factor).astype(out[name].dtype)
    return out
```

```python
import numpy as np
import concourse.bass as bass
from concourse import mybir
from contextlib import ExitStack

B, S, D, H, HD = 4, 1024, 128, 16, 8
E, F, TOPK = 64, 64, 8
T = B * S
NT = T // 128
HG = 4
NG = B * H // HG
NQT = S // 128
NPART = 3
ROWS_QK = NPART * NPART * HD
ROWS_BIAS = 2 * NQT * NPART
ROW_MAX = ROWS_QK + ROWS_BIAS
BETA = 48.0
STEPS = 2 * NQT
LAG = 2
NP_SLOTS = 4
TILES = NQT * HG
LOADS = 2 * NPART + 1
PARTS_OUT = 16 * NPART * 2
EPS = 1e-5


def host_constants():
    bf16 = mybir.dt.np(mybir.dt.bfloat16)

    def parts(v):
        out, rest = [], v.astype(np.float32)
        for _ in range(NPART):
            p = rest.astype(bf16)
            out.append(p)
            rest = rest - p.astype(np.float32)
        return out

    slopes = np.power(2.0, 8.0 * np.arange(0, -H, -1) / H).astype(np.float32)
    pos = np.arange(S)
    k_rows = np.zeros((H // HG, 128 - ROWS_QK, HG, S), bf16)
    q_rows = np.zeros((128 - ROWS_QK, HG, S), bf16)
    for j in range(NQT):
        side = np.sign(j - pos // 128).astype(np.float32)
        here = (pos // 128 == j).astype(np.float32)
        for c in range(NPART):
            q_rows[NPART * j + c] = here
            q_rows[NPART * (NQT + j) + c] = here * (pos - 128 * j)
        for h in range(H):
            s = slopes[h]
            line = np.where(side == 0, -BETA * s, side * s * (pos - 128 * j).astype(np.float32)).astype(np.float32)
            for c, (a, b) in enumerate(zip(parts(line), parts(-side * s))):
                k_rows[h // HG, NPART * j + c, h % HG] = a
                k_rows[h // HG, NPART * (NQT + j) + c, h % HG] = b
    k_rows[:, ROWS_BIAS:ROWS_BIAS + NPART] = 1.0
    dist = np.abs(np.arange(128)[:, None] - np.arange(128)[None, :])
    corr = slopes[:, None, None].astype(np.float64) * (BETA - dist)
    select = np.zeros((E // 2, 128, 128), np.float16)
    for e in range(E):
        select[e // 2, e, 64 * (e % 2):64 * (e % 2) + 64] = 1.0
        select[e // 2, E + e, 64 * (e % 2):64 * (e % 2) + 64] = 2.0 ** -12
    return {
        "k_rows": k_rows.reshape(H // HG, 128 - ROWS_QK, HG * S),
        "q_rows": q_rows.reshape(128 - ROWS_QK, HG, 2, S // 2).transpose(0, 2, 1, 3).reshape(-1, HG * S),
        "corr_add": corr.astype(np.float32),
        "corr_mul": np.ascontiguousarray(np.exp(corr).astype(np.float32).transpose(1, 0, 2)),
        "select": select,
        "ident32": np.eye(128, dtype=np.float32),
        "ident16": np.eye(128).astype(bf16),
        "identh": np.eye(128, dtype=np.float16),
    }


def build(nc, a, out):
    f32, bf16, f16 = mybir.dt.float32, mybir.dt.bfloat16, mybir.dt.float16
    ALU, ACT, AX = mybir.AluOpType, mybir.ActivationFunctionType, mybir.AxisListType
    ds = bass.ds
    ctx = ExitStack()
    with ctx:
        def sb(name, shape, dt=f32):
            return ctx.enter_context(nc.sbuf_tensor(name, shape, dt))

        def ps(name, shape, dt=f32):
            return ctx.enter_context(nc.psum_tensor(name, shape, dt))

        def sem(name):
            return ctx.enter_context(nc.semaphore(name))

        q_parts = nc.dram_tensor("q_parts", [NPART, NG, HD, HG * S], bf16)
        k_parts = nc.dram_tensor("k_parts", [NPART, NG, HD, HG * S], bf16)

        q_stack = sb("q_stack", [128, 3, HG * S], bf16)
        k_stack = sb("k_stack", [128, 3, HG * S], bf16)
        probs = sb("probs", [128, NP_SLOTS, HG, 512])
        v_all = sb("v_all", [128, NG, NQT, HG * HD])
        v_stage = sb("v_stage", [128, NQT, HG, 32])
        corr_add = sb("corr_add_sb", [128, HG, 15 * 128])
        corr_mul = sb("corr_mul_sb", [128, H, 128])
        junk = sb("junk", [128, 2, S], bf16)
        u_sb = sb("u_sb", [128, 2, 512])
        attn = sb("attn", [128, B, 2, 4, D])
        row_max = sb("row_max", [128, 2, 16])
        max_rest = sb("max_rest", [128, 16])
        max_parts = sb("max_parts", [128, 2, NPART, 16], bf16)
        max_rows = sb("max_rows", [NPART * 16, 2, 128], bf16)
        rden = sb("rden", [128, 2, 4, HG, 1])
        ident32 = sb("ident32_sb", [128, 128])
        ident16 = sb("ident16_sb", [128, 128], bf16)
        identh = sb("identh_sb", [128, 128], f16)
        w_qkv = sb("w_qkv", [128, 3 * D])
        b_q = sb("b_q", [128, 2])
        b_qs = sb("b_qs", [128, 2])
        b_v = sb("b_v", [128, D])
        part_sb = sb("part_sb", [128, 2, NPART, S], bf16)
        flat = probs[:, :, :, :].rearrange("p a b c -> p (a b c)")
        x_t = flat[:, 0:T]
        qk32 = flat[:, T:T + 2 * S].rearrange("p (a b) -> p a b", a=2)
        rest = flat[:, T + 2 * S:T + 4 * S].rearrange("p (a b) -> p a b", a=2)
        x1_t = flat[:, 0:T]
        x1 = flat[:, T:2 * T].rearrange("p (t d) -> p t d", d=D)
        w_out = sb("w_out", [128, D])
        b_out = sb("b_out", [128, D])
        cent = sb("cent", [128, E])
        e_bias = sb("e_bias", [128, E])
        ws_up = sb("ws_up", [128, F])
        ws_down = sb("ws_down", [F, D])
        t3 = q_stack[:, :, :].rearrange("p a b -> p (a b)").bitcast(f32)
        a_t = t3[:, 0:512]
        y_sb = t3[:, 512:1024].rearrange("p (t d) -> p t d", t=4)
        x_in = t3[:, 1024:2048].rearrange("p (a t d) -> p a t d", a=2, t=4)
        stats = t3[:, 2048:2072].rearrange("p (t d) -> p t d", t=4)
        mean_var = t3[:, 2080:2088].rearrange("p (t d) -> p t d", t=4)
        rstd = t3[:, 2096:2100]
        var_eps = t3[:, 2104:2108]
        std = t3[:, 2112:2116]
        rstd0 = t3[:, 2120:2124]
        newton = t3[:, 2128:2132]
        newton2 = t3[:, 2136:2140]
        biased = t3[:, 2304:2560].rearrange("p (t e) -> p t e", t=4)
        top8 = t3[:, 2560:2592].rearrange("p (t e) -> p t e", t=4)
        rep = t3[:, 2816:3072].rearrange("p (t e) -> p t e", t=4)
        mask = t3[:, 3072:3328].rearrange("p (t e) -> p t e", t=4)
        expn = t3[:, 3328:3584].rearrange("p (t e) -> p t e", t=4)
        sig = t3[:, 3584:3840].rearrange("p (t e) -> p t e", t=4)
        wsum = t3[:, 3840:3844]
        wrec = t3[:, 3844:3848]
        cw = t3[:, 3856:4112].rearrange("p (t e) -> p t e", t=4)
        cw_rest = t3[:, 4112:4368].rearrange("p (t e) -> p t e", t=4)
        cw_half = t3[:, 4368:4624].bitcast(f16).rearrange("p (t e) -> p t e", t=4)
        t4 = k_stack[:, :, :].rearrange("p a b -> p (a b)").bitcast(f32)
        cw_t = t4[:, 0:T // 2].bitcast(f16)
        hid = t4[:, 2048:3072].rearrange("p (a b) -> p a b", a=2)
        hid_w = t4[:, 3072:5120].rearrange("p (a b) -> p a b", a=4)
        y_t = t4[:, 5120:5632]
        w_up = sb("w_up", [128, 2, 128])
        w_down = sb("w_down", [128, 2, 128])
        w_sel = sb("w_sel", [128, 2, 128], f16)

        ring_a = ps("ring_a", [128, 2, S])
        ring_b = ps("ring_b", [128, 2, 512])
        ring_u = ps("ring_u", [128, 2, 512])

        ld_const = sem("ld_const")
        ld_x = sem("ld_x")
        zeroed = sem("zeroed")
        qk_full = sem("qk_full")
        qk_taken = sem("qk_taken")
        act_chain = sem("act_chain")
        rest1 = sem("rest1")
        mid = sem("mid")
        low = sem("low")
        parts_out = sem("parts_out")
        v_full = sem("v_full")
        v_taken = sem("v_taken")
        stacked = sem("stacked")
        corr_ld = [sem(f"corr_ld{h}") for h in range(HG)]
        a_full = sem("a_full")
        a_free = sem("a_free")
        dve_chain = sem("dve_chain")
        max_split = sem("max_split")
        max_in = sem("max_in")
        st_full = sem("st_full")
        exp_done = sem("exp_done")
        diag_done = sem("diag_done")
        v_staged = sem("v_staged")
        pv_done = sem("pv_done")
        u_taken = sem("u_taken")
        v_init = sem("v_init")

        x1_ready = sem("x1_ready")
        s3_ld = sem("s3_ld")
        at_full = sem("at_full")
        at_sb = sem("at_sb")
        pr_full = sem("pr_full")
        y_ready = sem("y_ready")
        x1t_full = sem("x1t_full")
        x1t_sb = sem("x1t_sb")
        aff_full = sem("aff_full")
        sig_exp = sem("sig_exp")
        cw_ready = sem("cw_ready")
        cwt_full = sem("cwt_full")
        cwt_sb = sem("cwt_sb")
        w_ld = [sem("w_ld0"), sem("w_ld1")]
        h_full = sem("h_full")
        h_act = sem("h_act")
        cb_full = sem("cb_full")
        hw_done = sem("hw_done")
        dn_done = sem("dn_done")
        sh_act = sem("sh_act")
        acc_full = sem("acc_full")
        acc_sb = sem("acc_sb")
        yt_full = sem("yt_full")
        y2_ready = sem("y2_ready")
        out_done = sem("out_done")
        var_ready = sem("var_ready")
        std_ready = sem("std_ready")
        waited = sem("waited")
        waited_pe = sem("waited_pe")

        block = ctx.enter_context(nc.Block())

        NCONST = 15

        def ring_step(s, first, last):
            e = []
            if s == 1:
                e.append(("max", 1))
            if s == 3 and not first:
                e.append(("u", 1))
            if s == 9 and not last:
                e.append(("max", 0))
            if s == 11:
                e.append(("u", 0))
            if not last:
                e += [("tile", 2 * s), ("tile", 2 * s + 1)]
            return e

        def ring_list(first, last):
            return [x for s in range(STEPS) for x in ring_step(s, first, last)]

        FULL = len(ring_list(False, False))
        START = TILES + 1

        def ring_base(i, first):
            return START if first else START - 1 + i * FULL

        def base_slot(first):
            return (START if first else START - 1) % 2

        def entry_of(kind, first, last):
            return ring_list(first, last).index(kind)

        def tile_of(k):
            u, r = divmod(k, TILES // 2)
            return 4 * u + r % 4, r // 4

        def q_at(u, h, pos):
            return (u * HG + h) * 512 + pos

        def diag_index(s):
            qh, kt = divmod(s, NQT)
            return None if kt // 4 != qh else (s if qh == 0 else s - 8)

        def wait_dn(half, pairs):
            return half * (E // 2) * 4 + pairs * 4

        def acc_view(q):
            return ring_a[:, q // 2, 512 * (q % 2):512 * (q % 2) + 512]

        @block.sync
        def _(sp):
            n = 0
            for dst, src in ((w_qkv[:, :], a["w_qkv_t"]), (ident32[:, :], a["ident32"]), (ident16[:, :], a["ident16"]),
                             (identh[:, :], a["identh"]), (b_q[:, :], a["b_qk"]),
                             (b_v[:, :], a["b_v"].to_broadcast([128, D])),
                             (corr_mul[:, :, :], a["corr_mul"]),
                             (w_out[:, :], a["w_out_t"]), (b_out[:, :], a["b_out"].to_broadcast([128, D])),
                             (cent[:, :], a["cent_t"]), (e_bias[:, :], a["e_bias"].to_broadcast([128, E])),
                             (ws_up[:, :], a["ws_up"]), (ws_down[:, :], a["ws_down"])):
                sp.dma_start(dst, src).then_inc(ld_const, 16)
                n += 1
                if n == 1:
                    for b in range(B):
                        sp.dma_start(x_t[:, b * S:(b + 1) * S], a["x_t"][:, b * S:(b + 1) * S]).then_inc(ld_x, 16)
            assert n == NCONST - 2
            for buf in range(3):
                sp.dma_start(q_stack[ROWS_QK:128, buf, :], a["q_rows"]).then_inc(ld_const, 16)

            for j in range(2 * B):
                b, isk = divmod(j, 2)
                sp.wait_ge(low, j + 1)
                sp.wait_ge(mid, j + 1)
                for c in range(NPART):
                    for u in range(2):
                        if isk:
                            dst = k_parts[c, 4 * b:4 * b + 4, :, :].rearrange("g d (h s) -> (g d) h s", h=HG
                                                                             )[:, :, 512 * u:512 * u + 512]
                        else:
                            dst = q_parts[c, 4 * b:4 * b + 4, :, 2048 * u:2048 * u + 2048].rearrange(
                                "g d (h s) -> (g d) h s", h=HG)
                        sp.dma_start(dst, part_sb[:, j % 2, c, 512 * u:512 * u + 512]).then_inc(parts_out, 16)
            sp.wait_ge(parts_out, PARTS_OUT * 2 * B)

            def load_stack(n):
                buf = n % 3
                for i in range(NPART):
                    r = NPART * HD * i
                    sp.dma_start(q_stack[r:r + NPART * HD, ds(buf, 1), :].rearrange("p a s -> p (a s)"),
                                 q_parts[i:i + 1, ds(n, 1), :, :].rearrange("c a d s -> (c a) d s")
                                 .to_broadcast([NPART, HD, HG * S])).then_inc(stacked, 16)
                    sp.dma_start(k_stack[r:r + NPART * HD, ds(buf, 1), :].rearrange("p a s -> p (a s)"),
                                 k_parts[:, ds(n, 1), :, :].rearrange("c a d s -> c (a d) s")).then_inc(stacked, 16)
                sp.dma_start(k_stack[ROWS_QK:128, ds(buf, 1), :].rearrange("p a s -> p (a s)"),
                             a["k_rows"][ds(n % 4, 1), :, :].rearrange("a p s -> p (a s)")).then_inc(stacked, 16)

            def load_corr(n, h):
                sp.dma_start(corr_add[:, h, 7 * 128:8 * 128],
                             a["corr_add"][ds((n % 4) * HG + h, 1), :, :].rearrange("a p k -> p (a k)")
                             ).then_inc(corr_ld[h], 16)

            def max_rows_in(n, u):
                buf = n % 3
                sp.dma_start(q_stack[ROW_MAX:ROW_MAX + NPART, ds(buf, 1), 2048 * u:2048 * u + 2048]
                             .rearrange("p a s -> p (a s)"), max_rows[:, u, :]).then_inc(max_in, 16)

            load_stack(0)
            sp.wait_ge(zeroed, 1)
            for h in range(HG):
                load_corr(0, h)
            sp.wait_ge(stacked, 16 * LOADS)
            load_stack(1)
            for h in range(HG - 1):
                sp.wait_ge(a_free, 20 + 4 * h)
                load_corr(1, h)
            sp.wait_ge(a_free, START)
            max_rows_in(0, 0)

            def iteration(i, first, last, load):
                base = ring_base(i, first)
                sp.wait_ge(a_free, base + entry_of(("max", 1), first, last) + 1)
                sp.wait_ge(max_in, (2 * i + 1) * 16)
                max_rows_in(i, 1)
                if not last:
                    load_corr(i + 1, HG - 1)
                if load:
                    if not first:
                        sp.wait_ge(st_full, i * STEPS * HG)
                    sp.wait_ge(stacked, (i + 2) * 16 * LOADS)
                    load_stack(i + 2)
                if not last:
                    for h in range(HG - 1):
                        if load:
                            sp.wait_ge(a_free, base + entry_of(("tile", 19 + 4 * h), first, last) + 1)
                            load_corr(i + 2, h)
                        if h == 0:
                            sp.wait_ge(a_free, base + entry_of(("max", 0), first, last) + 1)
                            sp.wait_ge(max_in, (2 * i + 2) * 16)
                            max_rows_in(i + 1, 0)

            iteration(0, True, False, True)
            with sp.Fori(1, NG - 2) as i:
                iteration(i, False, False, True)
            iteration(NG - 2, False, False, False)
            iteration(NG - 1, False, True, False)

            for c in range(NT // 4):
                if c == 0:
                    sp.wait_ge(st_full, NG * STEPS * HG)
                if c >= 2:
                    sp.wait_ge(y_ready, c - 1)
                sp.dma_start(x_in[:, c % 2, :, :],
                             a["x"][512 * c:512 * c + 512, :].rearrange("(t p) d -> p t d", p=128)
                             ).then_inc(s3_ld, 16)
                sp.wait_ge(s3_ld, 16 * (c + 1))

            def load_pair(half, pair, par, wait):
                if wait:
                    sp.wait_ge(dn_done, wait_dn(half, pair - 1))
                for dst, src in ((w_up, "w_up"), (w_down, "w_down"), (w_sel, "select")):
                    sp.dma_start(dst[:, par, :], a[src][ds(pair, 1), :, :].rearrange("a p n -> p (a n)")
                                 ).then_inc(w_ld[par], 16)

            for half in range(2):
                load_pair(half, 0, 0, half > 0)
                load_pair(half, 1, 1, half > 0)
                with sp.Fori(1, E // 4) as j:
                    for par in range(2):
                        load_pair(half, 2 * j + par, par, True)
                for q in range(4):
                    c = 4 * half + q
                    sp.wait_ge(y2_ready, c + 1)
                    if c:
                        sp.wait_ge(out_done, 16 * c)
                    sp.dma_start(out[512 * c:512 * c + 512, :].rearrange("(t p) d -> p t d", p=128),
                                 y_sb[:, :, :] if c % 2 == 0 else x_in[:, 0, :, :]).then_inc(out_done, 16)
            sp.wait_ge(out_done, 16 * 8)

        @block.tensor
        def _(pe):
            pe.wait_ge(ld_const, 16 * NCONST + 16)
            for j in range(2 * B):
                b, isk = divmod(j, 2)
                pe.wait_ge(ld_x, 16 * B)
                if j >= 2:
                    pe.wait_ge(qk_taken, j - 1)
                for n in range(2):
                    last = nc.tensor.matmul(ring_a[:, j % 2, 512 * n:512 * n + 512],
                                            w_qkv[:, D * isk:D * isk + D],
                                            x_t[:, b * S + 512 * n:b * S + 512 * n + 512], start=True, stop=True)
                last.then_inc(qk_full, 1)
                if j >= 2:
                    pe.wait_ge(v_taken, j - 1)
                for t in range(4):
                    last = nc.tensor.matmul(ring_b[:, j % 2, D * t:D * t + D],
                                            x_t[:, (4 * j + t) * 128:(4 * j + t + 1) * 128],
                                            w_qkv[:, 2 * D:3 * D], start=True, stop=True)
                last.then_inc(v_full, 1)

            def tile_half(n, k, slot, half):
                qt, h = tile_of(k)
                buf = n % 3
                return nc.tensor.matmul(
                    ring_a[:, slot, 512 * half:512 * half + 512],
                    q_stack[0:ROW_MAX, ds(buf, 1), q_at(qt // 4, h, 128 * (qt % 4)):q_at(qt // 4, h, 128 * (qt % 4)) + 128]
                    .rearrange("p a s -> p (a s)"),
                    k_stack[0:ROW_MAX, ds(buf, 1), h * S + 512 * half:h * S + 512 * half + 512].rearrange("p a s -> p (a s)"),
                    start=True, stop=True)

            def units(n_tile, i, entry, kind, x, slot, first):
                def free():
                    pe.wait_ge(a_free, entry - 1)
                if kind == "tile":
                    def one():
                        free()
                        tile_half(n_tile, x, slot, 0)
                    return [one, lambda: tile_half(n_tile, x, slot, 1).then_inc(a_full, 1)]
                if kind == "max":
                    def one():
                        free()
                        g = i if x == 1 else i + 1
                        pe.wait_ge(max_split, 2 * g + x + 1)
                        pe.sem_inc(waited_pe, 1)
                        nc.tensor.transpose(ring_a[0:NPART * 16, slot, 0:64].bitcast(bf16),
                                            max_parts[:, x, :, :].rearrange("p c n -> p (c n)"),
                                            ident16[:, :]).then_inc(a_full, 1)
                    return [one]

                def one():
                    free()
                    pe.wait_ge(u_taken, 2 * i + 1 - x)
                    for t in range(4):
                        last = nc.tensor.transpose(ring_a[:, slot, 128 * t:128 * t + 128],
                                                   u_sb[:, x, 128 * t:128 * t + 128], ident32[:, :])
                    last.then_inc(a_full, 1)
                return [one]

            def p_t_v(i, s, h):
                qh, kt = divmod(s, NQT)
                if h == 0:
                    if kt == 0:
                        if not isinstance(i, int) or 2 * i + qh >= 2:
                            pe.wait_ge(u_taken, 2 * i + qh - 1)
                    if s in (0, 4):
                        pe.wait_ge(v_staged, 2 * i + s // 4 + 1)
                    if diag_index(s) is not None:
                        pe.wait_ge(diag_done, 8 * i + diag_index(s) + 1)
                if diag_index(s) is None:
                    pe.wait_ge(exp_done, (STEPS * i + s) * HG + h + 1)
                last = nc.tensor.matmul(ring_u[32 * h:32 * h + 32, qh, :], v_stage[:, kt, h, :],
                                        probs[:, s % NP_SLOTS, h, :], start=kt == 0, stop=kt == NQT - 1)
                if h == HG - 1:
                    last.then_inc(pv_done, 1)

            pe.wait_ge(stacked, 16 * LOADS)
            pe.wait_ge(qk_taken, 2 * B)
            pe.wait_ge(v_taken, 2 * B)
            for k in range(TILES):
                if k >= 2:
                    pe.wait_ge(a_free, k - 1)
                tile_half(0, k, k % 2, 0)
                tile_half(0, k, k % 2, 1).then_inc(a_full, 1)
            units(0, -1, TILES, "max", 0, TILES % 2, True)[0]()

            def iteration(i, first, last):
                base, entry = ring_base(i, first), 0
                if not last:
                    pe.wait_ge(stacked, (i + 2) * 16 * LOADS)
                buf = i % 3
                for s in range(STEPS):
                    qh, kt = divmod(s, NQT)
                    work = []
                    for kind, x in ring_step(s, first, last):
                        work += units(i + 1, i, base + entry, kind, x, (base_slot(first) + entry) % 2, first)
                        entry += 1
                    if kt == 0:
                        pe.wait_ge(max_in, (2 * i + qh + 1) * 16)
                    for h in range(HG):
                        n = s * HG + h
                        if not (first and n < 2):
                            pe.wait_ge(exp_done, i * STEPS * HG + n - 1)
                        nc.tensor.matmul(
                            ring_b[:, h % 2, :],
                            k_stack[:, ds(buf, 1), h * S + 128 * kt:h * S + 128 * kt + 128].rearrange("p a s -> p (a s)"),
                            q_stack[:, ds(buf, 1), q_at(qh, h, 0):q_at(qh, h, 0) + 512].rearrange("p a s -> p (a s)"),
                            start=True, stop=True).then_inc(st_full, 1)
                        share = -(-len(work) // (HG - h)) if work else 0
                        for _ in range(share):
                            work.pop(0)()
                        if s >= LAG:
                            p_t_v(i, s - LAG, h)
                        elif not first:
                            p_t_v(i - 1, s - LAG + STEPS, h)

            iteration(0, True, False)
            with pe.Fori(1, NG - 1) as i:
                iteration(i, False, False)
            iteration(NG - 1, False, True)
            for s in range(STEPS - LAG, STEPS):
                for h in range(HG):
                    p_t_v(NG - 1, s, h)
            tail = ring_base(NG - 1, False) + len(ring_list(False, True))
            units(0, NG, tail, "u", 1, (base_slot(False) + len(ring_list(False, True))) % 2, False)[0]()
            last_entry = tail + 1

            pe.wait_ge(a_free, last_entry)
            for c in range(NT // 4):
                b, qh = divmod(c, 2)
                if c >= 1:
                    pe.wait_ge(at_sb, c)
                for t in range(4):
                    last = nc.tensor.transpose(ring_a[:, 0, 128 * t:128 * t + 128],
                                               attn[:, b, qh, t, :], ident32[:, :])
                last.then_inc(at_full, 1)
                pe.wait_ge(at_sb, c + 1)
                if c >= 1:
                    pe.wait_ge(y_ready, c)
                for t in range(4):
                    last = nc.tensor.matmul(ring_b[:, 0, 128 * t:128 * t + 128], a_t[:, 128 * t:128 * t + 128],
                                            w_out[:, :], start=True, stop=True)
                last.then_inc(pr_full, 1)
                pe.wait_ge(x1_ready, c + 1)
                for t in range(4):
                    last = nc.tensor.transpose(ring_a[:, 1, 128 * t:128 * t + 128], x1[:, 4 * c + t, :], ident32[:, :])
                last.then_inc(x1t_full, 1)
                pe.wait_ge(x1t_sb, c + 1)
            for c in range(NT // 4):
                if c >= 1:
                    pe.wait_ge(cw_ready, c)
                for t in range(4):
                    last = nc.tensor.matmul(ring_b[:, 1, E * t:E * t + E],
                                            x1_t[:, 512 * c + 128 * t:512 * c + 128 * t + 128],
                                            cent[:, :], start=True, stop=True)
                last.then_inc(aff_full, 1)
                pe.wait_ge(cw_ready, c + 1)
                for t in range(4):
                    last = nc.tensor.transpose(ring_u[:, 0, 64 * t:64 * t + 64].bitcast(f16), cw_half[:, t, :],
                                               identh[:, :])
                last.then_inc(cwt_full, 1)
                pe.wait_ge(cwt_sb, c + 1)

            acc = ring_a[:, :, :].rearrange("p a (b n) -> p (a b) n", b=2)

            def up(half, j, par, q, wait_free):
                unit = half * (E // 2) * 4 + (2 * j + par) * 4 + q
                if q == 0:
                    pe.wait_ge(w_ld[par], (half * (E // 4) + j + 1) * 48)
                if wait_free:
                    pe.wait_ge(h_act, unit - 1)
                tok = half * (T // 2) + 512 * q
                nc.tensor.matmul(ring_b[:, q % 2, :], w_up[:, par, :], x1_t[:, tok:tok + 512],
                                 start=True, stop=True).then_inc(h_full, 1)
                if wait_free:
                    pe.wait_ge(hw_done, unit - 1)
                nc.tensor.matmul(ring_u[:, q % 2, :], w_sel[:, par, :], cw_t[:, tok:tok + 512],
                                 start=True, stop=True).then_inc(cb_full, 1)

            def down(half, j, par, q, start):
                unit = half * (E // 2) * 4 + (2 * j + par) * 4 + q
                pe.wait_ge(hw_done, unit + 1)
                nc.tensor.matmul(acc[:, q, :], w_down[:, par, :], hid_w[:, q, :],
                                 start=start, stop=False).then_inc(dn_done, 1)

            def pairs(half, j, first):
                for u in range(8):
                    up(half, j, u // 4, u % 4, not (first and half == 0 and u < 2))
                    if u >= LAG:
                        down(half, j, (u - LAG) // 4, (u - LAG) % 4, first and u - LAG < 4)
                    elif not first:
                        down(half, j - 1, 1, u - LAG + 4, False)

            for half in range(2):
                if half:
                    pe.wait_ge(acc_sb, 4 * half)
                pairs(half, 0, True)
                with pe.Fori(1, E // 4) as j:
                    pairs(half, j, False)
                for q in (2, 3):
                    down(half, E // 4 - 1, 1, q, False)
                for q in range(4):
                    n = 4 * half + q
                    tok = half * (T // 2) + 512 * q
                    if q == 0:
                        pe.wait_ge(h_act, (half + 1) * (E // 2) * 4)
                    nc.tensor.matmul(ring_b[0:F, 0, :], ws_up[:, :], x1_t[:, tok:tok + 512],
                                     start=True, stop=True).then_inc(h_full, 1)
                    pe.wait_ge(sh_act, n + 1)
                    nc.tensor.matmul(acc[:, q, :], ws_down[:, :], hid[0:F, 0, :],
                                     start=False, stop=True).then_inc(acc_full, 1)
                for q in range(4):
                    n = 4 * half + q
                    pe.wait_ge(acc_sb, n + 1)
                    if q:
                        pe.wait_ge(y2_ready, n)
                    for t in range(4):
                        last = nc.tensor.transpose(ring_b[:, 1, 128 * t:128 * t + 128],
                                                   y_t[:, 128 * t:128 * t + 128], ident32[:, :])
                    last.then_inc(yt_full, 1)
                pe.wait_ge(y2_ready, 4 * half + 4)

        @block.scalar
        def _(act):
            scale = 1.0 / float(np.sqrt(HD))
            act.wait_ge(ld_const, 16 * NCONST + 16)
            nc.scalar.mul(b_qs[:, 0:1], b_q[:, 0:1], scale).then_inc(act_chain, 1)
            nc.scalar.copy(b_qs[:, 1:2], b_q[:, 1:2]).then_inc(act_chain, 1)
            act.wait_ge(act_chain, 2)

            def middle_part(j):
                act.wait_ge(rest1, j + 1)
                nc.scalar.copy(part_sb[:, j % 2, 1, :], rest[:, j % 2, :]).then_inc(mid, 1)

            for j in range(2 * B):
                isk = j % 2
                act.wait_ge(qk_full, j + 1)
                if j >= 2:
                    act.wait_ge(rest1, j - 1)
                    act.wait_ge(parts_out, PARTS_OUT * (j - 1))
                nc.scalar.activation(qk32[:, j % 2, :], ring_a[:, j % 2, :], ACT.Identity,
                                     bias=b_qs[:, isk:isk + 1], scale=1.0 if isk else scale).then_inc(act_chain, 1)
                act.wait_ge(act_chain, 3 + j)
                nc.scalar.copy(part_sb[:, j % 2, 0, :], qk32[:, j % 2, :]).then_inc(qk_taken, 1)
                if j >= 1:
                    middle_part(j - 1)
            middle_part(2 * B - 1)

            def take_u(i, qh, done=False):
                act.wait_ge(pv_done, STEPS * i + NQT * (qh + 1))
                if not isinstance(i, int) or i > 0:
                    act.wait_ge(a_full, START - 1 + FULL * (i - 1 + qh) + entry_of(("u", qh), False, done) + 1)
                nc.scalar.copy(u_sb[:, qh, :], ring_u[:, qh, :]).then_inc(u_taken, 1)

            def iteration(i, first, last):
                for s in range(STEPS):
                    for h in range(HG):
                        n = s * HG + h
                        act.wait_ge(st_full, i * STEPS * HG + n + 1)
                        if h == 0 and not (first and s < NP_SLOTS):
                            act.wait_ge(pv_done, STEPS * i + s - NP_SLOTS + 1)
                        nc.scalar.activation(probs[:, s % NP_SLOTS, h, :], ring_b[:, h % 2, :], ACT.Exp
                                             ).then_inc(exp_done, 1)
                    if s == 2 and not first:
                        take_u(i - 1, 1)
                    if s == 10:
                        take_u(i, 0)

            act.wait_ge(low, 2 * B)
            act.wait_ge(v_full, 2 * B)
            iteration(0, True, False)
            with act.Fori(1, NG - 1) as i:
                iteration(i, False, False)
            iteration(NG - 1, False, True)
            take_u(NG - 1, 1, True)

            def std_dev(n):
                act.wait_ge(var_ready, n + 1)
                nc.scalar.activation(std, var_eps, ACT.Sqrt).then_inc(std_ready, 1)

            for c in range(NT // 4):
                act.wait_ge(at_full, c + 1)
                if c >= 1:
                    act.wait_ge(pr_full, c)
                nc.scalar.copy(a_t, ring_a[:, 0, 0:512]).then_inc(at_sb, 1)
                std_dev(c)
                act.wait_ge(x1t_full, c + 1)
                nc.scalar.copy(x1_t[:, 512 * c:512 * c + 512], ring_a[:, 1, 0:512]).then_inc(x1t_sb, 1)
            for c in range(NT // 4):
                act.wait_ge(aff_full, c + 1)
                if c >= 1:
                    act.wait_ge(cw_ready, c)
                nc.scalar.activation(expn.rearrange("p t e -> p (t e)"), ring_b[:, 1, 0:256], ACT.Exp, scale=-1.0
                                     ).then_inc(sig_exp, 1)
                act.wait_ge(cwt_full, c + 1)
                nc.scalar.copy(cw_t[:, 512 * c:512 * c + 512], ring_u[:, 0, 0:256].bitcast(f16)).then_inc(cwt_sb, 1)

            def gate(half, j, par, q, first):
                unit = half * (E // 2) * 4 + (2 * j + par) * 4 + q
                act.wait_ge(h_full, unit + 4 * half + 1)
                if not first:
                    act.wait_ge(hw_done, unit - 1)
                nc.scalar.activation(hid[:, q % 2, :], ring_b[:, q % 2, :], ACT.Silu).then_inc(h_act, 1)

            for half in range(2):
                for u in range(8):
                    gate(half, 0, u // 4, u % 4, half == 0 and u < 2)
                with act.Fori(1, E // 4) as j:
                    for u in range(8):
                        gate(half, j, u // 4, u % 4, False)
                for q in range(4):
                    n = 4 * half + q
                    act.wait_ge(h_full, (half + 1) * (E // 2) * 4 + n + 1)
                    act.wait_ge(hw_done, (half + 1) * (E // 2) * 4)
                    nc.scalar.activation(hid[0:F, 0, :], ring_b[0:F, 0, :], ACT.Silu).then_inc(sh_act, 1)
                for q in range(4):
                    n = 4 * half + q
                    act.wait_ge(acc_full, n + 1)
                    if n >= 1:
                        act.wait_ge(yt_full, n)
                    nc.scalar.copy(y_t, acc_view(q)).then_inc(acc_sb, 1)
                    std_dev(NT // 4 + n)

        @block.vector
        def _(dve):
            def group_v(ap):
                return ap.rearrange("p t (g c) -> p t g c", g=H // HG)

            def low_part(j):
                dve.wait_ge(mid, j + 1)
                nc.vector.tensor_tensor(part_sb[:, j % 2, 2, :], rest[:, j % 2, :], part_sb[:, j % 2, 1, :],
                                        ALU.subtract).then_inc(low, 1)

            dve.wait_ge(ld_const, 16 * NCONST + 16)
            for j in range(2 * B):
                b, half = divmod(j, 2)
                dve.wait_ge(v_full, j + 1)
                nc.vector.tensor_tensor(
                    v_all[:, 4 * b:4 * b + 4, 4 * half:4 * half + 4, :].rearrange("p g t c -> p t g c"),
                    ring_b[:, j % 2, :].rearrange("p (t g c) -> p t g c", t=4, g=4),
                    b_v[:, :].rearrange("p (o g c) -> p o g c", o=1, g=4).to_broadcast([128, 4, 4, 32]),
                    ALU.add).then_inc(v_taken, 1)
                dve.wait_ge(qk_taken, j + 1)
                if j >= 2:
                    dve.wait_ge(mid, j - 1)
                nc.vector.tensor_tensor(rest[:, j % 2, :], qk32[:, j % 2, :], part_sb[:, j % 2, 0, :],
                                        ALU.subtract).then_inc(rest1, 1)
                if j >= 1:
                    low_part(j - 1)
            low_part(2 * B - 1)
            chain = 0

            def pass_a_tile(n, k, slot, entry):
                qt, h = tile_of(k)
                if k % 16 % 4 == 0:
                    dve.wait_ge(corr_ld[h], 16 * (n + 1))
                dve.wait_ge(a_full, entry + 1)
                dve.sem_inc(waited, 1)
                u = qt // 4
                col = 4 * h + qt % 4
                nc.vector.tensor_tensor_reduce(
                    out=junk[:, slot, :], in0=ring_a[:, slot, :],
                    in1=corr_add[:, h, 896 - 128 * qt:896 - 128 * qt + S],
                    scale=1.0, scalar=-3.0e38, op0=ALU.add, op1=ALU.max,
                    accum_out=row_max[:, u, col:col + 1]).then_inc(a_free, 1)

            def split_max(u, chain, entries):
                dve.wait_ge(a_free, entries)
                nc.vector.tensor_scalar(max_parts[:, u, 0, :], row_max[:, u, :], -1.0, None, ALU.mult
                                        ).then_inc(dve_chain, 1)
                dve.wait_ge(dve_chain, chain + 1)
                nc.vector.scalar_tensor_tensor(max_rest[:, :], row_max[:, u, :], -1.0, max_parts[:, u, 0, :],
                                               ALU.mult, ALU.subtract).then_inc(dve_chain, 1)
                dve.wait_ge(dve_chain, chain + 2)
                nc.vector.tensor_copy(max_parts[:, u, 1, :], max_rest[:, :]).then_inc(dve_chain, 1)
                dve.wait_ge(dve_chain, chain + 3)
                nc.vector.tensor_tensor(max_parts[:, u, 2, :], max_rest[:, :], max_parts[:, u, 1, :],
                                        ALU.subtract).then_inc(max_split, 1)

            def take_max(n, u, slot, entry, wait):
                dve.wait_ge(a_full, entry + 1)
                if wait:
                    dve.wait_ge(max_in, (2 * n + u - 1) * 16)
                nc.vector.tensor_copy(max_rows[:, u, :], ring_a[0:NPART * 16, slot, 0:64].bitcast(bf16)
                                      ).then_inc(a_free, 1)

            def take_out(n, u, slot, entry, chain):
                dve.wait_ge(a_full, entry + 1)
                v = ring_a[:, slot, 0:512].rearrange("p (t h c) -> p t h c", t=4, h=HG)
                nc.vector.reciprocal(rden[:, u, :, :, :], v[:, :, :, HD:HD + 1]).then_inc(dve_chain, 1)
                dve.wait_ge(dve_chain, chain + 1)
                nc.vector.tensor_tensor(
                    attn[:, ds(n // (H // HG), 1), u, :, ds((n % (H // HG)) * HG * HD, HG * HD)]
                    .rearrange("p a t (h c) -> p (a t) h c", h=HG),
                    v[:, :, :, 0:HD], rden[:, u, :, :, :].to_broadcast([128, 4, HG, HD]), ALU.mult
                ).then_inc(a_free, 1)

            dve.wait_ge(zeroed, 1)
            for k in range(TILES):
                pass_a_tile(0, k, k % 2, k)
                if k % 16 == 15:
                    split_max(k // 16, 3 * (k // 16), k + 1)
            take_max(0, 0, TILES % 2, TILES, False)
            CH0, CHF, CHFULL = 6, 7, 8

            def iteration(i, first, last):
                base, entry = ring_base(i, first), 0
                chain = CH0 if first else CH0 - 1 + i * CHFULL
                for s in range(STEPS):
                    for kind, x in ring_step(s, first, last):
                        slot = (base_slot(first) + entry) % 2
                        if kind == "tile":
                            pass_a_tile(i + 1, x, slot, base + entry)
                        elif kind == "max":
                            take_max(i if x else i + 1, x, slot, base + entry, not (first and x == 1))
                        else:
                            take_out(i - x, x, slot, base + entry, chain)
                            chain = chain + 1
                        entry += 1
                    if not last and s % NQT == NQT - 1:
                        split_max(s // NQT, chain, base + entry)
                        chain = chain + 3
                return chain

            iteration(0, True, False)
            with dve.Fori(1, NG - 1) as i:
                iteration(i, False, False)
            chain = iteration(NG - 1, False, True)
            tail = ring_base(NG - 1, False) + len(ring_list(False, True))
            take_out(NG - 1, 1, (base_slot(False) + len(ring_list(False, True))) % 2, tail, chain)
            chain += 1
            steps = [chain]
            ln_count = [0]

            def link(ins):
                steps[0] += 1
                ins.then_inc(dve_chain, 1)
                dve.wait_ge(dve_chain, steps[0])

            def layer_norm(src, dst, done):
                for t in range(4):
                    last = nc.vector.bn_stats(stats[:, t, :], src[:, t, :])
                link(last)
                for t in range(4):
                    last = nc.vector.bn_aggr(mean_var[:, t, :], stats[:, t, :])
                link(last)
                nc.vector.tensor_scalar(var_eps, mean_var[:, :, 1], EPS, None, ALU.add).then_inc(var_ready, 1)
                ln_count[0] += 1
                dve.wait_ge(std_ready, ln_count[0])
                link(nc.vector.reciprocal(rstd0, std))
                link(nc.vector.tensor_tensor(newton, rstd0, rstd0, ALU.mult))
                link(nc.vector.tensor_tensor(newton2, newton, var_eps, ALU.mult))
                link(nc.vector.tensor_scalar(newton, newton2, -0.5, 1.5, ALU.mult, ALU.add))
                link(nc.vector.tensor_tensor(rstd, newton, rstd0, ALU.mult))
                for t in range(4):
                    last = nc.vector.tensor_scalar(dst[:, t, :], src[:, t, :], mean_var[:, t, 0:1],
                                                   rstd[:, t:t + 1], ALU.subtract, ALU.mult)
                last.then_inc(done, 1)

            for c in range(NT // 4):
                dve.wait_ge(s3_ld, 16 * (c + 1))
                dve.wait_ge(pr_full, c + 1)
                link(nc.vector.tensor_tensor(y_sb, ring_b[:, 0, :].rearrange("p (t d) -> p t d", t=4),
                                             x_in[:, c % 2, :, :], ALU.add))
                nc.vector.tensor_tensor(y_sb, y_sb, b_out[:, :].rearrange("p (o d) -> p o d", o=1)
                                        .to_broadcast([128, 4, D]), ALU.add).then_inc(y_ready, 1)
                dve.wait_ge(y_ready, c + 1)
                layer_norm(y_sb, x1[:, 4 * c:4 * c + 4, :], x1_ready)
            for c in range(NT // 4):
                dve.wait_ge(aff_full, c + 1)
                dve.wait_ge(sig_exp, c + 1)
                link(nc.vector.tensor_tensor(biased, ring_b[:, 1, 0:256].rearrange("p (t e) -> p t e", t=4),
                                             e_bias[:, :].rearrange("p (o e) -> p o e", o=1)
                                             .to_broadcast([128, 4, E]), ALU.add))
                for t in range(4):
                    last = nc.vector.max(top8[:, t, :], biased[:, t, :])
                link(last)
                for t in range(4):
                    last = nc.vector.match_replace(rep[:, t, :], top8[:, t, :], biased[:, t, :], -3.0e38)
                link(last)
                link(nc.vector.tensor_tensor(mask, rep, biased, ALU.not_equal))
                link(nc.vector.tensor_scalar(sig, expn, 1.0, None, ALU.add))
                link(nc.vector.reciprocal(expn, sig))
                link(nc.vector.tensor_tensor(sig, expn, mask, ALU.mult))
                link(nc.vector.tensor_reduce(wsum, sig, AX.X, ALU.add))
                link(nc.vector.tensor_scalar(wrec, wsum, 1e-8, None, ALU.add))
                link(nc.vector.reciprocal(wsum, wrec))
                link(nc.vector.tensor_tensor(cw, sig, wsum.rearrange("p (t o) -> p t o", o=1)
                                             .to_broadcast([128, 4, E]), ALU.mult))
                if c >= 1:
                    dve.wait_ge(cwt_full, c)
                link(nc.vector.tensor_copy(cw_half[:, :, 0:E], cw))
                link(nc.vector.tensor_tensor(cw_rest, cw, cw_half[:, :, 0:E], ALU.subtract))
                nc.vector.tensor_scalar(cw_half[:, :, E:2 * E], cw_rest, 4096.0, None, ALU.mult
                                        ).then_inc(cw_ready, 1)

            def weigh(half, j, par, q, first):
                unit = half * (E // 2) * 4 + (2 * j + par) * 4 + q
                dve.wait_ge(h_act, unit + 1)
                dve.wait_ge(cb_full, unit + 1)
                if not first:
                    dve.wait_ge(dn_done, unit - 3)
                nc.vector.tensor_tensor(hid_w[:, q, :], ring_u[:, q % 2, :], hid[:, q % 2, :], ALU.mult
                                        ).then_inc(hw_done, 1)

            for half in range(2):
                for u in range(8):
                    weigh(half, 0, u // 4, u % 4, half == 0 and u < 4)
                with dve.Fori(1, E // 4) as j:
                    for u in range(8):
                        weigh(half, j, u // 4, u % 4, False)
                for q in range(4):
                    n = 4 * half + q
                    dst = y_sb if n % 2 == 0 else x_in[:, 0, :, :]
                    dve.wait_ge(yt_full, n + 1)
                    if n >= 2:
                        dve.wait_ge(out_done, 16 * (n - 1))
                    link(nc.vector.tensor_tensor(x_in[:, 1, :, :], ring_b[:, 1, :].rearrange("p (t d) -> p t d", t=4),
                                                 x1[:, 4 * n:4 * n + 4, :], ALU.add))
                    layer_norm(x_in[:, 1, :, :], dst, y2_ready)

        @block.gpsimd
        def _(pool):
            nc.gpsimd.memset(corr_add[:, :, :], 0.0).then_inc(zeroed, 1)
            nc.gpsimd.memset(v_stage[:, :, :, :], 0.0).then_inc(v_init, 1)
            pool.wait_ge(v_init, 1)
            nc.gpsimd.memset(v_stage[:, :, :, HD:HD + 1], 1.0).then_inc(v_init, 1)
            pool.wait_ge(v_init, 2)

            def stage_v(i, part):
                nc.gpsimd.tensor_copy(
                    v_stage[:, 4 * part:4 * part + 4, :, 0:HD],
                    v_all[:, ds(i, 1), 4 * part:4 * part + 4, :].rearrange("p a t (h c) -> p (a t) h c", h=HG)
                ).then_inc(v_staged, 1)

            pool.wait_ge(v_taken, 2 * B)
            pool.wait_ge(ld_const, 16 * NCONST + 16)
            stage_v(0, 0)
            stage_v(0, 1)

            def iteration(i, first, last):
                for s in range(STEPS):
                    if s == 2 and not first:
                        pool.wait_ge(pv_done, STEPS * i)
                        stage_v(i, 1)
                    if s == 14 and not last:
                        pool.wait_ge(pv_done, STEPS * i + 12)
                        stage_v(i + 1, 0)
                    d = diag_index(s)
                    if d is not None:
                        kt4 = s % 4
                        pool.wait_ge(exp_done, (STEPS * i + s + 1) * HG)
                        blk = probs[:, s % NP_SLOTS, :, 128 * kt4:128 * kt4 + 128]
                        nc.gpsimd.tensor_tensor(blk, blk, corr_mul[:, ds((i % 4) * HG, HG), :], ALU.mult
                                                ).then_inc(diag_done, 1)

            iteration(0, True, False)
            with pool.Fori(1, NG - 1) as i:
                iteration(i, False, False)
            iteration(NG - 1, False, True)


def kernel(L0_attn_x, L0_attn_W_qkv, L0_attn_b_qkv, L0_attn_W_out, L0_attn_b_out, L0_ffn_centroids,
           L0_ffn_expert_biases, L0_ffn_Ws_up, L0_ffn_Ws_down, L0_ffn_W_up, L0_ffn_W_down):
    import concourse.bacc as bacc
    from concourse.bass_utils import run_bass_kernel_spmd

    x = np.asarray(L0_attn_x).reshape(T, D)
    row = np.arange(D).reshape(H // HG, HG, HD).transpose(0, 2, 1).ravel()
    row = np.concatenate([row, D + row, 2 * D + np.arange(D)])
    w_qkv, b_qkv = np.asarray(L0_attn_W_qkv)[row], np.asarray(L0_attn_b_qkv)[row]
    host = {
        "x": x, "x_t": x.T, "w_qkv_t": w_qkv.T,
        "b_qk": b_qkv[0:2 * D].reshape(2, D).T, "b_v": b_qkv[2 * D:].reshape(1, D),
        "w_out_t": np.asarray(L0_attn_W_out).T, "b_out": np.asarray(L0_attn_b_out).reshape(1, D),
        "cent_t": np.asarray(L0_ffn_centroids).T, "e_bias": np.asarray(L0_ffn_expert_biases).reshape(1, E),
        "ws_up": np.asarray(L0_ffn_Ws_up), "ws_down": np.asarray(L0_ffn_Ws_down),
        "w_up": np.asarray(L0_ffn_W_up).reshape(E // 2, 2, D, F).transpose(0, 2, 1, 3).reshape(E // 2, D, 2 * F),
        "w_down": np.asarray(L0_ffn_W_down).reshape(E // 2, 2 * F, D),
        **host_constants(),
    }
    nc = bacc.Bacc("TRN2", target_bir_lowering=False, num_devices=1)
    nc.disable_value_cache = True
    arrays, aps = {}, {}
    for name, v in host.items():
        v = np.ascontiguousarray(v)
        arrays["in_" + name] = v
        aps[name] = nc.dram_tensor("in_" + name, v.shape, mybir.dt.from_np(v.dtype), kind="ExternalInput").ap()
    out = nc.dram_tensor("out_0", [T, D], mybir.dt.float32, kind="ExternalOutput").ap()
    build(nc, aps, out)
    r = run_bass_kernel_spmd(nc, [arrays], core_ids=[0])
    return r.results[0]["out_0"].reshape(B, S, D)
```

```python
import numpy as np
import concourse.bass as bass
from concourse import mybir
from contextlib import ExitStack

B, S, D, H, HD = 4, 1024, 128, 16, 8
E, F, TOPK = 64, 64, 8
T = B * S
NT = T // 128
HG = 4
NG = B * H // HG
NQT = S // 128
NPART = 3
ROWS_QK = NPART * NPART * HD
ROWS_BIAS = 2 * NQT * NPART
ROW_MAX = ROWS_QK + ROWS_BIAS
BETA = 48.0
STEPS = 2 * NQT
LAG = 2
NP_SLOTS = 4
TILES = NQT * HG
LOADS = 2 * NPART + 1
PARTS_OUT = 16 * NPART * 2
EPS = 1e-5


def host_constants():
    bf16 = mybir.dt.np(mybir.dt.bfloat16)

    def parts(v):
        out, rest = [], v.astype(np.float32)
        for _ in range(NPART):
            p = rest.astype(bf16)
            out.append(p)
            rest = rest - p.astype(np.float32)
        return out

    slopes = np.power(2.0, 8.0 * np.arange(0, -H, -1) / H).astype(np.float32)
    pos = np.arange(S)
    k_rows = np.zeros((H // HG, 128 - ROWS_QK, HG, S), bf16)
    q_rows = np.zeros((128 - ROWS_QK, HG, S), bf16)
    for j in range(NQT):
        side = np.sign(j - pos // 128).astype(np.float32)
        here = (pos // 128 == j).astype(np.float32)
        for c in range(NPART):
            q_rows[NPART * j + c] = here
            q_rows[NPART * (NQT + j) + c] = here * (pos - 128 * j)
        for h in range(H):
            s = slopes[h]
            line = np.where(side == 0, -BETA * s, side * s * (pos - 128 * j).astype(np.float32)).astype(np.float32)
            for c, (a, b) in enumerate(zip(parts(line), parts(-side * s))):
                k_rows[h // HG, NPART * j + c, h % HG] = a
                k_rows[h // HG, NPART * (NQT + j) + c, h % HG] = b
    k_rows[:, ROWS_BIAS:ROWS_BIAS + NPART] = 1.0
    dist = np.abs(np.arange(128)[:, None] - np.arange(128)[None, :])
    corr = slopes[:, None, None].astype(np.float64) * (BETA - dist)
    select = np.zeros((E // 2, 128, 128), np.float16)
    for e in range(E):
        select[e // 2, e, 64 * (e % 2):64 * (e % 2) + 64] = 1.0
        select[e // 2, E + e, 64 * (e % 2):64 * (e % 2) + 64] = 2.0 ** -12
    return {
        "k_rows": k_rows.reshape(H // HG, 128 - ROWS_QK, HG * S),
        "q_rows": q_rows.reshape(128 - ROWS_QK, HG, 2, S // 2).transpose(0, 2, 1, 3).reshape(-1, HG * S),
        "corr_add": corr.astype(np.float32),
        "corr_mul": np.ascontiguousarray(np.exp(corr).astype(np.float32).transpose(1, 0, 2)),
        "select": select,
        "ident32": np.eye(128, dtype=np.float32),
        "ident16": np.eye(128).astype(bf16),
        "identh": np.eye(128, dtype=np.float16),
    }


def build(nc, a, out):
    f32, bf16, f16, f32r = mybir.dt.float32, mybir.dt.bfloat16, mybir.dt.float16, mybir.dt.float32r
    ALU, ACT, AX = mybir.AluOpType, mybir.ActivationFunctionType, mybir.AxisListType
    ds = bass.ds
    ctx = ExitStack()
    with ctx:
        def sb(name, shape, dt=f32):
            return ctx.enter_context(nc.sbuf_tensor(name, shape, dt))

        def ps(name, shape, dt=f32):
            return ctx.enter_context(nc.psum_tensor(name, shape, dt))

        def sem(name):
            return ctx.enter_context(nc.semaphore(name))

        q_parts = nc.dram_tensor("q_parts", [NPART, NG, HD, HG * S], bf16)
        k_parts = nc.dram_tensor("k_parts", [NPART, NG, HD, HG * S], bf16)

        attn = sb("attn", [128, B, 2, 4, D])
        x1 = sb("x1", [128, NT, D])
        ident32 = sb("ident32_sb", [128, 128])
        ident16 = sb("ident16_sb", [128, 128], bf16)
        identh = sb("identh_sb", [128, 128], f16)
        w_out = sb("w_out", [128, D])
        b_out = sb("b_out", [128, D])
        cent = sb("cent", [128, E])
        e_bias = sb("e_bias", [128, E])

        early = ExitStack()

        def sb1(name, shape, dt=f32):
            return early.enter_context(nc.sbuf_tensor(name, shape, dt))

        q_stack = sb1("q_stack", [128, 3, HG * S], bf16)
        k_stack = sb1("k_stack", [128, 3, HG * S], bf16)
        probs = sb1("probs", [128, NP_SLOTS, HG, 512])
        v_all = sb1("v_all", [128, NG, NQT, HG * HD])
        v_stage = sb1("v_stage", [128, NQT, HG, 32])
        corr_add = sb1("corr_add_sb", [128, HG, 15 * 128])
        corr_mul = sb1("corr_mul_sb", [128, H, 128])
        junk = sb1("junk", [128, 2, S], bf16)
        u_sb = sb1("u_sb", [128, 2, 512])
        row_max = sb1("row_max", [128, 2, 16])
        max_rest = sb1("max_rest", [128, 16])
        max_parts = sb1("max_parts", [128, 2, NPART, 16], bf16)
        max_rows = sb1("max_rows", [NPART * 16, 2, 128], bf16)
        rden = sb1("rden", [128, 2, 4, HG, 1])
        w_qkv = sb1("w_qkv", [128, 3 * D])
        b_q = sb1("b_q", [128, 2])
        b_qs = sb1("b_qs", [128, 2])
        b_v = sb1("b_v", [1, D])
        ones = sb1("ones", [1, D])
        part_sb = sb1("part_sb", [128, 2, NPART, S], bf16)
        flat = probs[:, :, :, :].rearrange("p a b c -> p (a b c)")
        x_t = flat[:, 0:T]
        qk32 = flat[:, T:T + 2 * S].rearrange("p (a b) -> p a b", a=2)
        rest = flat[:, T + 2 * S:T + 4 * S].rearrange("p (a b) -> p a b", a=2)
        early.close()

        x_hi = sb("x_hi", [128, T], f32r)
        x_lo = sb("x_lo", [128, T], f32r)
        cw_t = sb("cw_t", [128, T], f16)
        cent_hi = sb("cent_hi", [128, E], f32r)
        cent_lo = sb("cent_lo", [128, E], f32r)
        a_t = sb("a_t", [128, 2, 512])
        stats = sb("stats", [128, NT, 6])
        mean_var = sb("mean_var", [128, NT, 2])
        var_eps = sb("var_eps", [128, NT])
        std = sb("std", [128, NT])
        rstd0 = sb("rstd0", [128, NT])
        newton = sb("newton", [128, NT])
        newton2 = sb("newton2", [128, NT])
        rstd = sb("rstd", [128, NT])
        biased = sb("biased", [128, 4, E])
        top8 = sb("top8", [128, 4, TOPK])
        marked = sb("marked", [128, 4, E])
        mask = sb("mask", [128, 4, E])
        sig = sb("sig", [128, 2, 4, E])
        sel_sig = sb("sel_sig", [128, 4, E])
        wsum = sb("wsum", [128, 4])
        wsum_eps = sb("wsum_eps", [128, 4])
        wrec = sb("wrec", [128, 4])
        cw = sb("cw", [128, 2, 4, E])
        cw_rest = sb("cw_rest", [128, 2, 4, E])
        cw_half = sb("cw_half", [128, 2, 4, 2 * E], f16)
        w_raw = sb("w_raw", [128, 2, 256])
        w_hi = sb("w_hi", [128, 2, 256], f32r)
        w_lo = sb("w_lo", [128, 2, 256], f32r)
        w_sel = sb("w_sel", [128, 2, 128], f16)
        ws_raw = sb("ws_raw", [128, 256])
        ws_hi = sb("ws_hi", [128, 256], f32r)
        ws_lo = sb("ws_lo", [128, 256], f32r)
        hid = sb("hid", [128, 2, 512])
        hid_w = sb("hid_w", [128, 2, 512])
        hid_hi = sb("hid_hi", [128, 4, 512], f32r)
        hid_lo = sb("hid_lo", [128, 4, 512], f32r)
        y_t = sb("y_t", [128, 2, 512])

        ring_a = ps("ring_a", [128, 2, S])
        ring_b = ps("ring_b", [128, 2, 512])
        ring_u = ps("ring_u", [128, 2, 512])

        ld_first = sem("ld_first")
        ld_const = sem("ld_const")
        ld_x = [sem(f"ld_x{b}") for b in range(B)]
        ld_res = sem("ld_res")
        zeroed = sem("zeroed")
        qk_full = sem("qk_full")
        qk_taken = sem("qk_taken")
        act_chain = sem("act_chain")
        rest_d = sem("rest_d")
        rest_p = sem("rest_p")
        mid = sem("mid")
        low_d = sem("low_d")
        low_p = sem("low_p")
        parts_out = [sem("q_parts_out"), sem("k_parts_out")]
        v_full = sem("v_full")
        v_taken = sem("v_taken")
        stacked = sem("stacked")
        corr_ld = [sem(f"corr_ld{h}") for h in range(HG)]
        a_full = sem("a_full")
        a_free = sem("a_free")
        dve_chain = sem("dve_chain")
        max_split = sem("max_split")
        max_in = sem("max_in")
        st_full = sem("st_full")
        exp_done = sem("exp_done")
        diag_done = sem("diag_done")
        v_staged = sem("v_staged")
        pv_done = sem("pv_done")
        u_taken = sem("u_taken")
        v_init = sem("v_init")

        res_ready = sem("res_ready")
        at_full = sem("at_full")
        at_sb = sem("at_sb")
        pr_full = sem("pr_full")
        pr_taken = sem("pr_taken")
        var_ready = sem("var_ready")
        std_ready = sem("std_ready")
        normed = sem("normed")
        xt_full = sem("xt_full")
        xt_hi = sem("xt_hi")
        xt_lo = sem("xt_lo")
        cent_split = sem("cent_split")
        aff_full = sem("aff_full")
        sig_done = sem("sig_done")
        aff_taken = sem("aff_taken")
        cw_done = sem("cw_done")
        pool_chain = sem("pool_chain")
        cw_split = sem("cw_split")
        cwt_full = sem("cwt_full")
        cwt_sb = sem("cwt_sb")
        w_ld = [sem("w_ld0"), sem("w_ld1")]
        ws_ld = sem("ws_ld")
        w_hi_done = sem("w_hi_done")
        w_split = sem("w_split")
        ws_split = sem("ws_split")
        h_full = sem("h_full")
        h_act = sem("h_act")
        cb_full = sem("cb_full")
        hw_done = sem("hw_done")
        hi_done = sem("hi_done")
        lo_done = sem("lo_done")
        dn_done = sem("dn_done")
        acc_sb = sem("acc_sb")
        yt_full = sem("yt_full")
        yt_taken = sem("yt_taken")
        y_ready = sem("y_ready")
        out_done = sem("out_done")
        waited = sem("waited")
        waited_pe = sem("waited_pe")
        waited_pool = sem("waited_pool")

        block = ctx.enter_context(nc.Block())

        LD_CONST = 11 * 16
        N_CHUNK = NT // 4
        U_HALF = (E // 2 + 1) * 4
        DOWN_LAG = 3

        def ring_step(s, first, last):
            e = []
            if s == 1:
                e.append(("max", 1))
            if s == 3 and not first:
                e.append(("u", 1))
            if s == 9 and not last:
                e.append(("max", 0))
            if s == 11:
                e.append(("u", 0))
            if not last:
                e += [("tile", 2 * s), ("tile", 2 * s + 1)]
            return e

        def ring_list(first, last):
            return [x for s in range(STEPS) for x in ring_step(s, first, last)]

        FULL = len(ring_list(False, False))
        START = TILES + 1

        def ring_base(i, first):
            return START if first else START - 1 + i * FULL

        def base_slot(first):
            return (START if first else START - 1) % 2

        def entry_of(kind, first, last):
            return ring_list(first, last).index(kind)

        LAST_ENTRY = START - 1 + (NG - 1) * FULL + len(ring_list(False, True)) + 1

        def tile_of(k):
            u, r = divmod(k, TILES // 2)
            return 4 * u + r % 4, r // 4

        def q_at(u, h, pos):
            return (u * HG + h) * 512 + pos

        def diag_index(s):
            qh, kt = divmod(s, NQT)
            return None if kt // 4 != qh else (s if qh == 0 else s - 8)

        acc = ring_a[:, :, :].rearrange("p a (b n) -> p (a b) n", b=2)

        @block.sync
        def _(sp):
            for dst, src in ((w_qkv[:, :], a["w_qkv_t"]), (b_q[:, :], a["b_qk"]), (b_v[:, :], a["b_v"])):
                sp.dma_start(dst, src).then_inc(ld_first, 16)
            for b in range(B):
                for u in range(2):
                    at = b * S + 512 * u
                    sp.dma_start(x_t[:, at:at + 512], a["x_t"][:, at:at + 512]).then_inc(ld_x[b], 16)
            for buf in range(3):
                sp.dma_start(q_stack[ROWS_QK:128, buf, :], a["q_rows"]).then_inc(ld_const, 16)
            for dst, src in ((ident32[:, :], a["ident32"]), (ident16[:, :], a["ident16"]), (identh[:, :], a["identh"]),
                             (corr_mul[:, :, :], a["corr_mul"]),
                             (w_out[:, :], a["w_out_t"]), (b_out[:, :], a["b_out"].to_broadcast([128, D])),
                             (cent[:, :], a["cent_t"]), (e_bias[:, :], a["e_bias"].to_broadcast([128, E]))):
                sp.dma_start(dst, src).then_inc(ld_const, 16)

            def parts_to_dram(j):
                b, isk = divmod(j, 2)
                for c in range(NPART):
                    for u in range(2):
                        if isk:
                            dst = k_parts[c, 4 * b:4 * b + 4, :, :].rearrange("g d (h s) -> (g d) h s", h=HG
                                                                             )[:, :, 512 * u:512 * u + 512]
                        else:
                            dst = q_parts[c, 4 * b:4 * b + 4, :, 2048 * u:2048 * u + 2048].rearrange(
                                "g d (h s) -> (g d) h s", h=HG)
                        sp.dma_start(dst, part_sb[:, j % 2, c, 512 * u:512 * u + 512]).then_inc(parts_out[isk], 16)

            for j in range(2):
                sp.wait_ge(low_d, j + 1)
                parts_to_dram(j)
            for isk in range(2):
                sp.wait_ge(parts_out[isk], PARTS_OUT)

            def load_stack(n):
                buf = n % 3
                for i in range(NPART):
                    r = NPART * HD * i
                    sp.dma_start(q_stack[r:r + NPART * HD, ds(buf, 1), :].rearrange("p a s -> p (a s)"),
                                 q_parts[i:i + 1, ds(n, 1), :, :].rearrange("c a d s -> (c a) d s")
                                 .to_broadcast([NPART, HD, HG * S])).then_inc(stacked, 16)
                    sp.dma_start(k_stack[r:r + NPART * HD, ds(buf, 1), :].rearrange("p a s -> p (a s)"),
                                 k_parts[:, ds(n, 1), :, :].rearrange("c a d s -> c (a d) s")).then_inc(stacked, 16)
                sp.dma_start(k_stack[ROWS_QK:128, ds(buf, 1), :].rearrange("p a s -> p (a s)"),
                             a["k_rows"][ds(n % 4, 1), :, :].rearrange("a p s -> p (a s)")).then_inc(stacked, 16)

            def load_corr(n, h):
                sp.dma_start(corr_add[:, h, 7 * 128:8 * 128],
                             a["corr_add"][ds((n % 4) * HG + h, 1), :, :].rearrange("a p k -> p (a k)")
                             ).then_inc(corr_ld[h], 16)

            def max_rows_in(n, u):
                buf = n % 3
                sp.dma_start(q_stack[ROW_MAX:ROW_MAX + NPART, ds(buf, 1), 2048 * u:2048 * u + 2048]
                             .rearrange("p a s -> p (a s)"), max_rows[:, u, :]).then_inc(max_in, 16)

            load_stack(0)
            sp.wait_ge(zeroed, 1)
            for h in range(HG):
                load_corr(0, h)
            sp.wait_ge(stacked, 16 * LOADS)
            load_stack(1)
            for j in range(2, 2 * B):
                sp.wait_ge(low_p, j - 1)
                sp.wait_ge(parts_out[j % 2], PARTS_OUT * (j // 2))
                parts_to_dram(j)
            for c in range(N_CHUNK):
                sp.dma_start(x1[:, 4 * c:4 * c + 4, :],
                             a["x"][512 * c:512 * c + 512, :].rearrange("(t p) d -> p t d", p=128)
                             ).then_inc(ld_res, 16)
            for isk in range(2):
                sp.wait_ge(parts_out[isk], PARTS_OUT * B)
            for h in range(HG - 1):
                sp.wait_ge(a_free, 20 + 4 * h)
                load_corr(1, h)
            sp.wait_ge(a_free, START)
            max_rows_in(0, 0)

            def iteration(i, first, last, load):
                base = ring_base(i, first)
                sp.wait_ge(a_free, base + entry_of(("max", 1), first, last) + 1)
                sp.wait_ge(max_in, (2 * i + 1) * 16)
                max_rows_in(i, 1)
                if not last:
                    load_corr(i + 1, HG - 1)
                if load:
                    if not first:
                        sp.wait_ge(st_full, i * STEPS * HG)
                    sp.wait_ge(stacked, (i + 2) * 16 * LOADS)
                    load_stack(i + 2)
                if not last:
                    for h in range(HG - 1):
                        if load:
                            sp.wait_ge(a_free, base + entry_of(("tile", 19 + 4 * h), first, last) + 1)
                            load_corr(i + 2, h)
                        if h == 0:
                            sp.wait_ge(a_free, base + entry_of(("max", 0), first, last) + 1)
                            sp.wait_ge(max_in, (2 * i + 2) * 16)
                            max_rows_in(i + 1, 0)

            iteration(0, True, False, True)
            with sp.Fori(1, NG - 2) as i:
                iteration(i, False, False, True)
            iteration(NG - 2, False, False, False)
            iteration(NG - 1, False, True, False)

            sp.wait_ge(a_free, LAST_ENTRY)
            sp.dma_start(ws_raw[:, :], a["w_shared"]).then_inc(ws_ld, 16)

            def load_pair(half, pair, par, first):
                if not first:
                    sp.wait_ge(w_split, half * (E // 2) + pair - 1)
                    sp.wait_ge(cb_full, (half * (E // 2) + pair - 1) * 4)
                sp.dma_start(w_raw[:, par, :], a["w_pairs"][ds(pair, 1), :, :].rearrange("a p n -> p (a n)")
                             ).then_inc(w_ld[par], 16)
                sp.dma_start(w_sel[:, par, :], a["select"][ds(pair, 1), :, :].rearrange("a p n -> p (a n)")
                             ).then_inc(w_ld[par], 16)

            for half in range(2):
                load_pair(half, 0, 0, half == 0)
                load_pair(half, 1, 1, half == 0)
                with sp.Fori(1, E // 4) as j:
                    for par in range(2):
                        load_pair(half, 2 * j + par, par, False)
                for q in range(4):
                    c = 4 * half + q
                    sp.wait_ge(y_ready, c + 1)
                    sp.dma_start(out[512 * c:512 * c + 512, :].rearrange("(t p) d -> p t d", p=128),
                                 x1[:, 4 * c:4 * c + 4, :]).then_inc(out_done, 16)
            sp.wait_ge(out_done, 16 * N_CHUNK)

        @block.tensor
        def _(pe):
            def project_qk(j):
                b, isk = divmod(j, 2)
                if j < 2:
                    psum = ring_a[:, j, :]
                else:
                    psum = ring_b[:, :, :].rearrange("p a b -> p (a b)")
                    if j > 2:
                        pe.wait_ge(qk_taken, j)
                pe.wait_ge(ld_x[b], 32)
                for n in range(2):
                    last = nc.tensor.matmul(psum[:, 512 * n:512 * n + 512], w_qkv[:, D * isk:D * isk + D],
                                            x_t[:, b * S + 512 * n:b * S + 512 * n + 512], start=True, stop=True)
                last.then_inc(qk_full, 1)

            def project_v(j):
                if j >= 2:
                    pe.wait_ge(v_taken, j - 1)
                pe.wait_ge(ld_x[j // 2], 32)
                for t in range(4):
                    nc.tensor.matmul(ring_u[:, j % 2, D * t:D * t + D], x_t[:, (4 * j + t) * 128:(4 * j + t + 1) * 128],
                                     w_qkv[:, 2 * D:3 * D], start=True, stop=False)
                    last = nc.tensor.matmul(ring_u[:, j % 2, D * t:D * t + D], ones[:, :], b_v[:, :],
                                            start=False, stop=True)
                last.then_inc(v_full, 1)

            pe.wait_ge(ld_first, 48)
            pe.wait_ge(zeroed, 2)
            project_qk(0)
            project_qk(1)
            project_v(0)
            project_v(1)

            def tile_half(n, k, slot, half):
                qt, h = tile_of(k)
                buf = n % 3
                return nc.tensor.matmul(
                    ring_a[:, slot, 512 * half:512 * half + 512],
                    q_stack[0:ROW_MAX, ds(buf, 1), q_at(qt // 4, h, 128 * (qt % 4)):q_at(qt // 4, h, 128 * (qt % 4)) + 128]
                    .rearrange("p a s -> p (a s)"),
                    k_stack[0:ROW_MAX, ds(buf, 1), h * S + 512 * half:h * S + 512 * half + 512].rearrange("p a s -> p (a s)"),
                    start=True, stop=True)

            def units(n_tile, i, entry, kind, x, slot, first):
                def free():
                    pe.wait_ge(a_free, entry - 1)
                if kind == "tile":
                    def one():
                        free()
                        tile_half(n_tile, x, slot, 0)
                    return [one, lambda: tile_half(n_tile, x, slot, 1).then_inc(a_full, 1)]
                if kind == "max":
                    def one():
                        free()
                        g = i if x == 1 else i + 1
                        pe.wait_ge(max_split, 2 * g + x + 1)
                        pe.sem_inc(waited_pe, 1)
                        nc.tensor.transpose(ring_a[0:NPART * 16, slot, 0:64].bitcast(bf16),
                                            max_parts[:, x, :, :].rearrange("p c n -> p (c n)"),
                                            ident16[:, :]).then_inc(a_full, 1)
                    return [one]

                def one():
                    free()
                    pe.wait_ge(u_taken, 2 * i + 1 - x)
                    for t in range(4):
                        last = nc.tensor.transpose(ring_a[:, slot, 128 * t:128 * t + 128],
                                                   u_sb[:, x, 128 * t:128 * t + 128], ident32[:, :])
                    last.then_inc(a_full, 1)
                return [one]

            def p_t_v(i, s, h):
                qh, kt = divmod(s, NQT)
                if h == 0:
                    if kt == 0:
                        if not isinstance(i, int) or 2 * i + qh >= 2:
                            pe.wait_ge(u_taken, 2 * i + qh - 1)
                    if s in (0, 4):
                        pe.wait_ge(v_staged, 2 * i + s // 4 + 1)
                    if diag_index(s) is not None:
                        pe.wait_ge(diag_done, 8 * i + diag_index(s) + 1)
                if diag_index(s) is None:
                    pe.wait_ge(exp_done, (STEPS * i + s) * HG + h + 1)
                last = nc.tensor.matmul(ring_u[32 * h:32 * h + 32, qh, :], v_stage[:, kt, h, :],
                                        probs[:, s % NP_SLOTS, h, :], start=kt == 0, stop=kt == NQT - 1)
                if h == HG - 1:
                    last.then_inc(pv_done, 1)

            pe.wait_ge(stacked, 16 * LOADS)
            pe.wait_ge(qk_taken, 2)
            others = [lambda j=j: project_qk(j) for j in range(2, 2 * B)]
            for n, j in enumerate(range(2, 2 * B)):
                others.insert(2 * n + 1, lambda j=j: project_v(j))
            for k in range(TILES):
                if k >= 2:
                    pe.wait_ge(a_free, k - 1)
                tile_half(0, k, k % 2, 0)
                tile_half(0, k, k % 2, 1).then_inc(a_full, 1)
                if k % 2 and others:
                    others.pop(0)()
            pe.wait_ge(qk_taken, 2 * B)
            pe.wait_ge(v_taken, 2 * B)
            units(0, -1, TILES, "max", 0, TILES % 2, True)[0]()

            def iteration(i, first, last):
                base, entry = ring_base(i, first), 0
                if not last:
                    pe.wait_ge(stacked, (i + 2) * 16 * LOADS)
                buf = i % 3
                for s in range(STEPS):
                    qh, kt = divmod(s, NQT)
                    work = []
                    for kind, x in ring_step(s, first, last):
                        work += units(i + 1, i, base + entry, kind, x, (base_slot(first) + entry) % 2, first)
                        entry += 1
                    if kt == 0:
                        pe.wait_ge(max_in, (2 * i + qh + 1) * 16)

                    def scores(h):
                        n = s * HG + h
                        if not (first and n < 2):
                            pe.wait_ge(exp_done, i * STEPS * HG + n - 1)
                        nc.tensor.matmul(
                            ring_b[:, h % 2, :],
                            k_stack[:, ds(buf, 1), h * S + 128 * kt:h * S + 128 * kt + 128].rearrange("p a s -> p (a s)"),
                            q_stack[:, ds(buf, 1), q_at(qh, h, 0):q_at(qh, h, 0) + 512].rearrange("p a s -> p (a s)"),
                            start=True, stop=True).then_inc(st_full, 1)

                    scores(0)
                    scores(1)
                    for h in range(HG):
                        if s >= LAG:
                            p_t_v(i, s - LAG, h)
                        elif not first:
                            p_t_v(i - 1, s - LAG + STEPS, h)
                    scores(2)
                    scores(3)
                    for call in work:
                        call()

            iteration(0, True, False)
            for i in range(1, NG - 1):
                iteration(i, False, False)
            iteration(NG - 1, False, True)
            for s in range(STEPS - LAG, STEPS):
                for h in range(HG):
                    p_t_v(NG - 1, s, h)
            units(0, NG, LAST_ENTRY - 1, "u", 1, (LAST_ENTRY - 1) % 2, False)[0]()

            pe.wait_ge(a_free, LAST_ENTRY)
            for c in range(N_CHUNK + 1):
                if c < N_CHUNK:
                    if c >= 2:
                        pe.wait_ge(at_sb, c - 1)
                    for t in range(4):
                        last = nc.tensor.transpose(ring_b[:, c % 2, 128 * t:128 * t + 128],
                                                   attn[:, c // 2, c % 2, t, :], ident32[:, :])
                    last.then_inc(at_full, 1)
                if c >= 1:
                    n = c - 1
                    pe.wait_ge(at_sb, n + 1)
                    if n >= 2:
                        pe.wait_ge(pr_taken, n - 1)
                    for t in range(4):
                        last = nc.tensor.matmul(ring_u[:, n % 2, 128 * t:128 * t + 128],
                                                a_t[:, n % 2, 128 * t:128 * t + 128], w_out[:, :],
                                                start=True, stop=True)
                    last.then_inc(pr_full, 1)
            pe.wait_ge(pr_taken, N_CHUNK)
            pe.wait_ge(cent_split, 2)
            for c in range(N_CHUNK + 3):
                if c < N_CHUNK:
                    pe.wait_ge(normed, c + 1)
                    if c >= 2:
                        pe.wait_ge(xt_lo, c - 1)
                    for t in range(4):
                        last = nc.tensor.transpose(ring_b[:, c % 2, 128 * t:128 * t + 128], x1[:, 4 * c + t, :],
                                                   ident32[:, :])
                    last.then_inc(xt_full, 1)
                n = c - 1
                if 0 <= n < N_CHUNK:
                    pe.wait_ge(xt_lo, n + 1)
                    if n >= 2:
                        pe.wait_ge(aff_taken, n - 1)
                    for t in range(4):
                        tok = slice(512 * n + 128 * t, 512 * n + 128 * t + 128)
                        for m, (x, w) in enumerate(((x_hi, cent_hi), (x_hi, cent_lo), (x_lo, cent_hi))):
                            last = nc.tensor.matmul(ring_u[:, n % 2, E * t:E * t + E], x[:, tok], w[:, :],
                                                    start=m == 0, stop=m == 2)
                    last.then_inc(aff_full, 1)
                n = c - 3
                if n >= 0:
                    pe.wait_ge(cw_split, n + 1)
                    if n >= 2:
                        pe.wait_ge(cwt_sb, n - 1)
                    for t in range(4):
                        last = nc.tensor.transpose(ring_a[:, n % 2, 64 * t:64 * t + 64].bitcast(f16),
                                                   cw_half[:, n % 2, t, :], identh[:, :])
                    last.then_inc(cwt_full, 1)
            pe.wait_ge(cwt_sb, N_CHUNK)

            def up(half, pair, par, q, skip):
                p = E // 2 if pair is None else pair
                unit = half * U_HALF + p * 4 + q
                hi, lo = (ws_hi[:, 0:128], ws_lo[:, 0:128]) if pair is None else (w_hi[:, par, 0:128], w_lo[:, par, 0:128])
                if q == 0:
                    if pair is None:
                        pe.wait_ge(ws_split, 2)
                    else:
                        pe.wait_ge(w_split, half * (E // 2) + pair + 1)
                if not skip:
                    pe.wait_ge(h_act, unit - 1)
                tok = half * (T // 2) + 512 * q
                for m, (w, x) in enumerate(((hi, x_hi), (hi, x_lo), (lo, x_hi))):
                    last = nc.tensor.matmul(ring_b[:, q % 2, :], w, x[:, tok:tok + 512], start=m == 0, stop=m == 2)
                last.then_inc(h_full, 1)
                if pair is not None:
                    if not skip:
                        pe.wait_ge(hw_done, unit - 1)
                    nc.tensor.matmul(ring_u[:, q % 2, :], w_sel[:, par, :], cw_t[:, tok:tok + 512],
                                     start=True, stop=True).then_inc(cb_full, 1)

            def down(half, pair, par, q, start=False, stop=False):
                p = E // 2 if pair is None else pair
                unit = half * U_HALF + p * 4 + q
                hi, lo = (ws_hi[:, 128:256], ws_lo[:, 128:256]) if pair is None else (
                    w_hi[:, par, 128:256], w_lo[:, par, 128:256])
                pe.wait_ge(lo_done, unit + 1)
                for m, (w, h) in enumerate(((hi, hid_hi), (lo, hid_hi), (hi, hid_lo))):
                    last = nc.tensor.matmul(acc[:, q, :], w, h[:, q, :], start=start and m == 0, stop=stop and m == 2)
                last.then_inc(dn_done, 1)

            def pairs(half, j, first):
                for u in range(8):
                    up(half, 2 * j + u // 4, u // 4, u % 4, first and half == 0 and u < 2)
                    if u >= DOWN_LAG:
                        d = u - DOWN_LAG
                        down(half, 2 * j + d // 4, d // 4, d % 4, start=first and d < 4)
                    elif not first:
                        down(half, 2 * j - 1, 1, u - DOWN_LAG + 4)

            for half in range(2):
                if half:
                    pe.wait_ge(acc_sb, 4)
                    pe.wait_ge(yt_taken, 4)
                pairs(half, 0, True)
                with pe.Fori(1, E // 4) as j:
                    pairs(half, j, False)
                for q in range(4):
                    up(half, None, 0, q, False)
                    if q < DOWN_LAG:
                        down(half, E // 2 - 1, 1, q - DOWN_LAG + 4)
                    else:
                        down(half, None, 0, q - DOWN_LAG, stop=True)
                for q in range(4 - DOWN_LAG, 4):
                    down(half, None, 0, q, stop=True)
                for q in range(4):
                    n = 4 * half + q
                    pe.wait_ge(acc_sb, n + 1)
                    if q >= 2:
                        pe.wait_ge(yt_taken, n - 1)
                    for t in range(4):
                        last = nc.tensor.transpose(ring_b[:, q % 2, 128 * t:128 * t + 128],
                                                   y_t[:, q % 2, 128 * t:128 * t + 128], ident32[:, :])
                    last.then_inc(yt_full, 1)

        @block.scalar
        def _(act):
            scale = 1.0 / float(np.sqrt(HD))
            act.wait_ge(ld_first, 48)
            nc.scalar.mul(b_qs[:, 0:1], b_q[:, 0:1], scale).then_inc(act_chain, 1)
            nc.scalar.copy(b_qs[:, 1:2], b_q[:, 1:2]).then_inc(act_chain, 1)
            act.wait_ge(act_chain, 2)

            def take_qk(j):
                isk = j % 2
                act.wait_ge(qk_full, j + 1)
                if j >= 2:
                    if j < 4:
                        act.wait_ge(rest_d, j - 1)
                    else:
                        act.wait_ge(rest_p, j - 3)
                    act.wait_ge(parts_out[isk], PARTS_OUT * (j // 2))
                psum = ring_a[:, j, :] if j < 2 else ring_b[:, :, :].rearrange("p a b -> p (a b)")
                nc.scalar.activation(qk32[:, j % 2, :], psum, ACT.Identity,
                                     bias=b_qs[:, isk:isk + 1], scale=1.0 if isk else scale).then_inc(act_chain, 1)
                act.wait_ge(act_chain, 3 + j)
                nc.scalar.copy(part_sb[:, j % 2, 0, :], qk32[:, j % 2, :]).then_inc(qk_taken, 1)

            def middle_part(j):
                if j < 2:
                    act.wait_ge(rest_d, j + 1)
                else:
                    act.wait_ge(rest_p, j - 1)
                nc.scalar.copy(part_sb[:, j % 2, 1, :], rest[:, j % 2, :]).then_inc(mid, 1)

            def take_v(j):
                b, half = divmod(j, 2)
                act.wait_ge(v_full, j + 1)
                nc.scalar.copy(v_all[:, 4 * b:4 * b + 4, 4 * half:4 * half + 4, :].rearrange("p g t c -> p t g c"),
                               ring_u[:, j % 2, :].rearrange("p (t g c) -> p t g c", t=4, g=4)).then_inc(v_taken, 1)

            take_qk(0)
            take_qk(1)
            middle_part(0)
            middle_part(1)
            take_v(0)
            take_v(1)
            for j in range(2, 2 * B):
                take_qk(j)
                take_v(j)
                middle_part(j)

            def take_u(i, qh, done=False):
                act.wait_ge(pv_done, STEPS * i + NQT * (qh + 1))
                if not isinstance(i, int) or i > 0:
                    act.wait_ge(a_full, START - 1 + FULL * (i - 1 + qh) + entry_of(("u", qh), False, done) + 1)
                nc.scalar.copy(u_sb[:, qh, :], ring_u[:, qh, :]).then_inc(u_taken, 1)

            def iteration(i, first, last):
                for s in range(STEPS):
                    for h in range(HG):
                        n = s * HG + h
                        act.wait_ge(st_full, i * STEPS * HG + n + 1)
                        if h == 0 and not (first and s < NP_SLOTS):
                            act.wait_ge(pv_done, STEPS * i + s - NP_SLOTS + 1)
                        nc.scalar.activation(probs[:, s % NP_SLOTS, h, :], ring_b[:, h % 2, :], ACT.Exp
                                             ).then_inc(exp_done, 1)
                    if s == 2 and not first:
                        take_u(i - 1, 1)
                    if s == 10:
                        take_u(i, 0)

            act.wait_ge(low_p, 2 * B - 2)
            iteration(0, True, False)
            with act.Fori(1, NG - 1) as i:
                iteration(i, False, False)
            iteration(NG - 1, False, True)
            take_u(NG - 1, 1, True)

            act.wait_ge(a_free, LAST_ENTRY)

            def std_dev(n, tiles):
                act.wait_ge(var_ready, n + 1)
                nc.scalar.activation(std[:, tiles], var_eps[:, tiles], ACT.Sqrt).then_inc(std_ready, 1)

            for c in range(N_CHUNK):
                act.wait_ge(at_full, c + 1)
                if c >= 2:
                    act.wait_ge(pr_full, c - 1)
                nc.scalar.copy(a_t[:, c % 2, :], ring_b[:, c % 2, :]).then_inc(at_sb, 1)
            std_dev(0, slice(0, NT))
            for c in range(N_CHUNK + 3):
                if c < N_CHUNK:
                    act.wait_ge(xt_full, c + 1)
                    nc.scalar.copy(x_hi[:, 512 * c:512 * c + 512], ring_b[:, c % 2, :]).then_inc(xt_hi, 1)
                n = c - 1
                if 0 <= n < N_CHUNK:
                    act.wait_ge(aff_full, n + 1)
                    if n >= 2:
                        act.wait_ge(cw_done, n - 1)
                    nc.scalar.activation(sig[:, n % 2, :, :].rearrange("p t e -> p (t e)"), ring_u[:, n % 2, 0:4 * E],
                                         ACT.Sigmoid).then_inc(sig_done, 1)
                n = c - 3
                if n >= 0:
                    act.wait_ge(cwt_full, n + 1)
                    nc.scalar.copy(cw_t[:, 512 * n:512 * n + 512], ring_a[:, n % 2, 0:256].bitcast(f16)
                                   ).then_inc(cwt_sb, 1)

            def gate(unit, q, skip):
                act.wait_ge(h_full, unit + 1)
                if not skip:
                    act.wait_ge(hw_done, unit - 1)
                nc.scalar.activation(hid[:, q % 2, :], ring_b[:, q % 2, :], ACT.Silu).then_inc(h_act, 1)

            def high(unit, q, skip):
                act.wait_ge(hw_done, unit + 1)
                if not skip:
                    act.wait_ge(dn_done, unit - 3)
                nc.scalar.copy(hid_hi[:, q, :], hid_w[:, q % 2, :]).then_inc(hi_done, 1)

            def units(half, base, n, first):
                for u in range(n):
                    gate(base + u, u % 4, first and half == 0 and u < 2)
                    if not (first and u == 0):
                        high(base + u - 1, (u - 1) % 4, first and half == 0 and u < 5)

            for half in range(2):
                units(half, half * U_HALF, 8, True)
                with act.Fori(1, E // 4) as j:
                    units(half, half * U_HALF + 8 * j, 8, False)
                units(half, half * U_HALF + 2 * E, 4, False)
                high((half + 1) * U_HALF - 1, 3, False)
                for q in range(4):
                    n = 4 * half + q
                    act.wait_ge(dn_done, (half + 1) * U_HALF - 3 + q)
                    if q >= 2:
                        act.wait_ge(yt_full, n - 1)
                    elif half:
                        act.wait_ge(yt_full, n - 3)
                    nc.scalar.copy(y_t[:, q % 2, :], acc[:, q, :]).then_inc(acc_sb, 1)
                std_dev(half + 1, slice(16 * half, 16 * half + 16))

        @block.vector
        def _(dve):
            for j in range(2):
                dve.wait_ge(qk_taken, j + 1)
                nc.vector.tensor_tensor(rest[:, j, :], qk32[:, j, :], part_sb[:, j, 0, :],
                                        ALU.subtract).then_inc(rest_d, 1)
            for j in range(2):
                dve.wait_ge(mid, j + 1)
                nc.vector.tensor_tensor(part_sb[:, j, 2, :], rest[:, j, :], part_sb[:, j, 1, :],
                                        ALU.subtract).then_inc(low_d, 1)

            def pass_a_tile(n, k, slot, entry):
                qt, h = tile_of(k)
                if k % 16 % 4 == 0:
                    dve.wait_ge(corr_ld[h], 16 * (n + 1))
                dve.wait_ge(a_full, entry + 1)
                dve.sem_inc(waited, 1)
                u = qt // 4
                col = 4 * h + qt % 4
                nc.vector.tensor_tensor_reduce(
                    out=junk[:, slot, :], in0=ring_a[:, slot, :],
                    in1=corr_add[:, h, 896 - 128 * qt:896 - 128 * qt + S],
                    scale=1.0, scalar=-3.0e38, op0=ALU.add, op1=ALU.max,
                    accum_out=row_max[:, u, col:col + 1]).then_inc(a_free, 1)

            def split_max(u, chain, entries):
                dve.wait_ge(a_free, entries)
                nc.vector.tensor_scalar(max_parts[:, u, 0, :], row_max[:, u, :], -1.0, None, ALU.mult
                                        ).then_inc(dve_chain, 1)
                dve.wait_ge(dve_chain, chain + 1)
                nc.vector.scalar_tensor_tensor(max_rest[:, :], row_max[:, u, :], -1.0, max_parts[:, u, 0, :],
                                               ALU.mult, ALU.subtract).then_inc(dve_chain, 1)
                dve.wait_ge(dve_chain, chain + 2)
                nc.vector.tensor_copy(max_parts[:, u, 1, :], max_rest[:, :]).then_inc(dve_chain, 1)
                dve.wait_ge(dve_chain, chain + 3)
                nc.vector.tensor_tensor(max_parts[:, u, 2, :], max_rest[:, :], max_parts[:, u, 1, :],
                                        ALU.subtract).then_inc(max_split, 1)

            def take_max(n, u, slot, entry, wait):
                dve.wait_ge(a_full, entry + 1)
                if wait:
                    dve.wait_ge(max_in, (2 * n + u - 1) * 16)
                nc.vector.tensor_copy(max_rows[:, u, :], ring_a[0:NPART * 16, slot, 0:64].bitcast(bf16)
                                      ).then_inc(a_free, 1)

            def take_out(n, u, slot, entry, chain):
                dve.wait_ge(a_full, entry + 1)
                v = ring_a[:, slot, 0:512].rearrange("p (t h c) -> p t h c", t=4, h=HG)
                nc.vector.reciprocal(rden[:, u, :, :, :], v[:, :, :, HD:HD + 1]).then_inc(dve_chain, 1)
                dve.wait_ge(dve_chain, chain + 1)
                nc.vector.tensor_tensor(
                    attn[:, ds(n // (H // HG), 1), u, :, ds((n % (H // HG)) * HG * HD, HG * HD)]
                    .rearrange("p a t (h c) -> p (a t) h c", h=HG),
                    v[:, :, :, 0:HD], rden[:, u, :, :, :].to_broadcast([128, 4, HG, HD]), ALU.mult
                ).then_inc(a_free, 1)

            dve.wait_ge(zeroed, 1)
            for k in range(TILES):
                pass_a_tile(0, k, k % 2, k)
                if k % 16 == 15:
                    split_max(k // 16, 3 * (k // 16), k + 1)
            take_max(0, 0, TILES % 2, TILES, False)
            CH0, CHF, CHFULL = 6, 7, 8

            def iteration(i, first, last):
                base, entry = ring_base(i, first), 0
                chain = CH0 if first else CH0 - 1 + i * CHFULL
                for s in range(STEPS):
                    for kind, x in ring_step(s, first, last):
                        slot = (base_slot(first) + entry) % 2
                        if kind == "tile":
                            pass_a_tile(i + 1, x, slot, base + entry)
                        elif kind == "max":
                            take_max(i if x else i + 1, x, slot, base + entry, not (first and x == 1))
                        else:
                            take_out(i - x, x, slot, base + entry, chain)
                            chain = chain + 1
                        entry += 1
                    if not last and s % NQT == NQT - 1:
                        split_max(s // NQT, chain, base + entry)
                        chain = chain + 3
                return chain

            iteration(0, True, False)
            with dve.Fori(1, NG - 1) as i:
                iteration(i, False, False)
            chain = iteration(NG - 1, False, True)
            take_out(NG - 1, 1, (LAST_ENTRY - 1) % 2, LAST_ENTRY - 1, chain)
            chain += 1
            steps = [chain]
            dve.wait_ge(a_free, LAST_ENTRY)

            def link(ins):
                steps[0] += 1
                ins.then_inc(dve_chain, 1)
                dve.wait_ge(dve_chain, steps[0])

            def add_residual(c, psum, done):
                rows = x1[:, 4 * c:4 * c + 4, :]
                nc.vector.tensor_tensor(rows, psum.rearrange("p (t d) -> p t d", t=4), rows, ALU.add).then_inc(done, 1)
                dve.wait_ge(done, c + 1)
                for t in range(4 * c, 4 * c + 4):
                    last = nc.vector.bn_stats(stats[:, t, :], x1[:, t, :])
                link(last)
                for t in range(4 * c, 4 * c + 4):
                    last = nc.vector.bn_aggr(mean_var[:, t, :], stats[:, t, :])
                return last

            def inverse_std(n, ts):
                nc.vector.tensor_scalar(var_eps[:, ts], mean_var[:, ts, 1], EPS, None, ALU.add).then_inc(var_ready, 1)
                dve.wait_ge(std_ready, n + 1)
                link(nc.vector.reciprocal(rstd0[:, ts], std[:, ts]))
                link(nc.vector.tensor_tensor(newton[:, ts], rstd0[:, ts], rstd0[:, ts], ALU.mult))
                link(nc.vector.tensor_tensor(newton2[:, ts], newton[:, ts], var_eps[:, ts], ALU.mult))
                link(nc.vector.tensor_scalar(newton[:, ts], newton2[:, ts], -0.5, 1.5, ALU.mult, ALU.add))
                link(nc.vector.tensor_tensor(rstd[:, ts], newton[:, ts], rstd0[:, ts], ALU.mult))

            def normalise(c, done):
                for t in range(4 * c, 4 * c + 4):
                    last = nc.vector.tensor_scalar(x1[:, t, :], x1[:, t, :], mean_var[:, t, 0:1], rstd[:, t:t + 1],
                                                   ALU.subtract, ALU.mult)
                last.then_inc(done, 1)

            def bank(row):
                return row.rearrange("p (o e) -> p o e", o=1).to_broadcast([128, 4, E])

            def per_tile(col):
                return col.rearrange("p (t o) -> p t o", o=1).to_broadcast([128, 4, E])

            def route(c):
                dve.wait_ge(aff_full, c + 1)
                dve.wait_ge(sig_done, c + 1)
                aff = ring_u[:, c % 2, 0:4 * E].rearrange("p (t e) -> p t e", t=4)
                nc.vector.tensor_tensor(biased[:, :, :], aff, bank(e_bias[:, :]), ALU.add).then_inc(aff_taken, 1)
                dve.wait_ge(aff_taken, c + 1)
                for t in range(4):
                    last = nc.vector.max(top8[:, t, :], biased[:, t, :])
                link(last)
                for t in range(4):
                    last = nc.vector.match_replace(marked[:, t, :], top8[:, t, :], biased[:, t, :], -3.0e38)
                link(last)
                link(nc.vector.tensor_tensor(mask[:, :, :], marked[:, :, :], biased[:, :, :], ALU.not_equal))
                link(nc.vector.tensor_tensor(sel_sig[:, :, :], sig[:, c % 2, :, :], mask[:, :, :], ALU.mult))
                link(nc.vector.tensor_reduce(wsum[:, :], sel_sig[:, :, :], AX.X, ALU.add))
                link(nc.vector.tensor_scalar(wsum_eps[:, :], wsum[:, :], 1e-8, None, ALU.add))
                link(nc.vector.reciprocal(wrec[:, :], wsum_eps[:, :]))
                if c >= 2:
                    dve.wait_ge(cw_split, c - 1)
                nc.vector.tensor_tensor(cw[:, c % 2, :, :], sel_sig[:, :, :], per_tile(wrec[:, :]), ALU.mult
                                        ).then_inc(cw_done, 1)
                dve.wait_ge(cw_done, c + 1)

            for c in range(N_CHUNK):
                dve.wait_ge(res_ready, c + 1)
                dve.wait_ge(pr_full, c + 1)
                link(add_residual(c, ring_u[:, c % 2, :], pr_taken))
            inverse_std(0, slice(0, NT))
            for c in range(N_CHUNK + 2):
                if c < N_CHUNK:
                    normalise(c, normed)
                n = c - 1
                if 0 <= n < N_CHUNK:
                    dve.wait_ge(xt_hi, n + 1)
                    nc.vector.tensor_tensor(x_lo[:, 512 * n:512 * n + 512], ring_b[:, n % 2, :],
                                            x_hi[:, 512 * n:512 * n + 512].bitcast(f32), ALU.subtract).then_inc(xt_lo, 1)
                n = c - 2
                if n >= 0:
                    route(n)

            def weigh(unit, cb, q):
                dve.wait_ge(h_act, unit + 1)
                if cb is None:
                    nc.vector.tensor_copy(hid_w[:, q % 2, :], hid[:, q % 2, :]).then_inc(hw_done, 1)
                else:
                    dve.wait_ge(cb_full, cb + 1)
                    nc.vector.tensor_tensor(hid_w[:, q % 2, :], ring_u[:, q % 2, :], hid[:, q % 2, :], ALU.mult
                                            ).then_inc(hw_done, 1)

            def low(unit, q, skip):
                dve.wait_ge(hi_done, unit + 1)
                if not skip:
                    dve.wait_ge(dn_done, unit - 3)
                nc.vector.tensor_tensor(hid_lo[:, q, :], hid_w[:, q % 2, :], hid_hi[:, q, :].bitcast(f32),
                                        ALU.subtract).then_inc(lo_done, 1)

            def units(half, base, cb, n, first):
                for u in range(n):
                    if not (first and u < 2):
                        dve.wait_ge(lo_done, base + u - 1)
                    weigh(base + u, None if cb is None else cb + u, u % 4)
                    if not (first and u == 0):
                        low(base + u - 1, (u - 1) % 4, first and half == 0 and u < 5)

            for half in range(2):
                units(half, half * U_HALF, half * 2 * E, 8, True)
                with dve.Fori(1, E // 4) as j:
                    units(half, half * U_HALF + 8 * j, half * 2 * E + 8 * j, 8, False)
                units(half, half * U_HALF + 2 * E, None, 4, False)
                low((half + 1) * U_HALF - 1, 3, False)
                for q in range(4):
                    n = 4 * half + q
                    dve.wait_ge(yt_full, n + 1)
                    link(add_residual(n, ring_b[:, q % 2, :], yt_taken))
                inverse_std(half + 1, slice(16 * half, 16 * half + 16))
                for q in range(4):
                    normalise(4 * half + q, y_ready)

        @block.gpsimd
        def _(pool):
            nc.gpsimd.memset(ones[:, :], 1.0).then_inc(zeroed, 1)
            nc.gpsimd.memset(corr_add[:, :, :], 0.0).then_inc(zeroed, 1)
            nc.gpsimd.memset(v_stage[:, :, :, :], 0.0).then_inc(v_init, 1)
            pool.wait_ge(v_init, 1)
            nc.gpsimd.memset(v_stage[:, :, :, HD:HD + 1], 1.0).then_inc(v_init, 1)
            pool.wait_ge(v_init, 2)

            for j in range(2, 2 * B):
                pool.wait_ge(qk_taken, j + 1)
                if j < 4:
                    pool.wait_ge(low_d, j - 1)
                nc.gpsimd.tensor_tensor(rest[:, j % 2, :], qk32[:, j % 2, :], part_sb[:, j % 2, 0, :],
                                        ALU.subtract).then_inc(rest_p, 1)
                pool.wait_ge(mid, j + 1)
                nc.gpsimd.tensor_tensor(part_sb[:, j % 2, 2, :], rest[:, j % 2, :], part_sb[:, j % 2, 1, :],
                                        ALU.subtract).then_inc(low_p, 1)

            def stage_v(i, part):
                pool.sem_inc(waited_pool, 1)
                nc.gpsimd.tensor_copy(
                    v_stage[:, 4 * part:4 * part + 4, :, 0:HD],
                    v_all[:, ds(i, 1), 4 * part:4 * part + 4, :].rearrange("p a t (h c) -> p (a t) h c", h=HG)
                ).then_inc(v_staged, 1)

            pool.wait_ge(v_taken, 2 * B)
            pool.wait_ge(ld_const, LD_CONST)
            stage_v(0, 0)
            stage_v(0, 1)

            def iteration(i, first, last):
                for s in range(STEPS):
                    if s == 2 and not first:
                        pool.wait_ge(pv_done, STEPS * i)
                        stage_v(i, 1)
                    if s == 14 and not last:
                        pool.wait_ge(pv_done, STEPS * i + 12)
                        stage_v(i + 1, 0)
                    d = diag_index(s)
                    if d is not None:
                        kt4 = s % 4
                        pool.wait_ge(exp_done, (STEPS * i + s + 1) * HG)
                        blk = probs[:, s % NP_SLOTS, :, 128 * kt4:128 * kt4 + 128]
                        nc.gpsimd.tensor_tensor(blk, blk, corr_mul[:, ds((i % 4) * HG, HG), :], ALU.mult
                                                ).then_inc(diag_done, 1)

            iteration(0, True, False)
            with pool.Fori(1, NG - 1) as i:
                iteration(i, False, False)
            iteration(NG - 1, False, True)

            for c in range(N_CHUNK):
                if c == 0:
                    pool.wait_ge(ld_res, 16 * N_CHUNK)
                nc.gpsimd.tensor_tensor(x1[:, 4 * c:4 * c + 4, :], x1[:, 4 * c:4 * c + 4, :],
                                        b_out[:, :].rearrange("p (o d) -> p o d", o=1).to_broadcast([128, 4, D]),
                                        ALU.add).then_inc(res_ready, 1)
            pool.wait_ge(a_free, LAST_ENTRY)

            nc.gpsimd.tensor_copy(cent_hi[:, :], cent[:, :]).then_inc(cent_split, 1)
            pool.wait_ge(cent_split, 1)
            nc.gpsimd.tensor_tensor(cent_lo[:, :], cent[:, :], cent_hi[:, :].bitcast(f32), ALU.subtract
                                    ).then_inc(cent_split, 1)
            pool.wait_ge(ws_ld, 16)
            nc.gpsimd.tensor_copy(ws_hi[:, :], ws_raw[:, :]).then_inc(ws_split, 1)
            pool.wait_ge(ws_split, 1)
            nc.gpsimd.tensor_tensor(ws_lo[:, :], ws_raw[:, :], ws_hi[:, :].bitcast(f32), ALU.subtract
                                    ).then_inc(ws_split, 1)
            for c in range(N_CHUNK):
                pool.wait_ge(cw_done, c + 1)
                if c >= 2:
                    pool.wait_ge(cwt_full, c - 1)
                nc.gpsimd.tensor_copy(cw_half[:, c % 2, :, 0:E], cw[:, c % 2, :, :]).then_inc(pool_chain, 1)
                pool.wait_ge(pool_chain, 2 * c + 1)
                nc.gpsimd.tensor_tensor(cw_rest[:, c % 2, :, :], cw[:, c % 2, :, :], cw_half[:, c % 2, :, 0:E],
                                        ALU.subtract).then_inc(pool_chain, 1)
                pool.wait_ge(pool_chain, 2 * c + 2)
                nc.gpsimd.tensor_scalar(cw_half[:, c % 2, :, E:2 * E], cw_rest[:, c % 2, :, :], 4096.0, None, ALU.mult
                                        ).then_inc(cw_split, 1)

            def split_pair(half, j, par, first):
                n = half * (E // 2) + 2 * j + par
                pool.wait_ge(w_ld[par], (half * (E // 4) + j + 1) * 32)
                if not first:
                    if isinstance(j, int):
                        pool.wait_ge(dn_done, half * U_HALF - 4)
                    else:
                        pool.wait_ge(dn_done, half * U_HALF + (2 * j + par - 1) * 4)
                pool.sem_inc(waited_pool, 1)
                nc.gpsimd.tensor_copy(w_hi[:, par, :], w_raw[:, par, :]).then_inc(w_hi_done, 1)
                pool.wait_ge(w_hi_done, n + 1)
                nc.gpsimd.tensor_tensor(w_lo[:, par, :], w_raw[:, par, :], w_hi[:, par, :].bitcast(f32), ALU.subtract
                                        ).then_inc(w_split, 1)

            for half in range(2):
                for par in range(2):
                    split_pair(half, 0, par, half == 0)
                with pool.Fori(1, E // 4) as j:
                    for par in range(2):
                        split_pair(half, j, par, False)


def kernel(L0_attn_x, L0_attn_W_qkv, L0_attn_b_qkv, L0_attn_W_out, L0_attn_b_out, L0_ffn_centroids,
           L0_ffn_expert_biases, L0_ffn_Ws_up, L0_ffn_Ws_down, L0_ffn_W_up, L0_ffn_W_down):
    import concourse.bacc as bacc
    from concourse.bass_utils import run_bass_kernel_spmd

    x = np.asarray(L0_attn_x).reshape(T, D)
    row = np.arange(D).reshape(H // HG, HG, HD).transpose(0, 2, 1).ravel()
    row = np.concatenate([row, D + row, 2 * D + np.arange(D)])
    w_qkv, b_qkv = np.asarray(L0_attn_W_qkv)[row], np.asarray(L0_attn_b_qkv)[row]
    pairs = np.concatenate([
        np.asarray(L0_ffn_W_up).reshape(E // 2, 2, D, F).transpose(0, 2, 1, 3).reshape(E // 2, D, 2 * F),
        np.asarray(L0_ffn_W_down).reshape(E // 2, 2 * F, D)], axis=2)
    shared = np.zeros((D, 2 * F + D), np.float32)
    shared[:, 0:F] = np.asarray(L0_ffn_Ws_up)
    shared[0:F, 2 * F:] = np.asarray(L0_ffn_Ws_down)
    host = {
        "x": x, "x_t": x.T, "w_qkv_t": w_qkv.T,
        "b_qk": b_qkv[0:2 * D].reshape(2, D).T, "b_v": b_qkv[2 * D:].reshape(1, D),
        "w_out_t": np.asarray(L0_attn_W_out).T, "b_out": np.asarray(L0_attn_b_out).reshape(1, D),
        "cent_t": np.asarray(L0_ffn_centroids).T, "e_bias": np.asarray(L0_ffn_expert_biases).reshape(1, E),
        "w_shared": shared, "w_pairs": pairs,
        **host_constants(),
    }
    nc = bacc.Bacc("TRN2", target_bir_lowering=False, num_devices=1)
    nc.disable_value_cache = True
    arrays, aps = {}, {}
    for name, v in host.items():
        v = np.ascontiguousarray(v)
        arrays["in_" + name] = v
        aps[name] = nc.dram_tensor("in_" + name, v.shape, mybir.dt.from_np(v.dtype), kind="ExternalInput").ap()
    out = nc.dram_tensor("out_0", [T, D], mybir.dt.float32, kind="ExternalOutput").ap()
    build(nc, aps, out)
    r = run_bass_kernel_spmd(nc, [arrays], core_ids=[0])
    return r.results[0]["out_0"].reshape(B, S, D)
```

```python
import numpy as np
import concourse.bass as bass
from concourse import mybir
from contextlib import ExitStack

B, S, D, H, HD = 4, 1024, 128, 16, 8
E, F, TOPK = 64, 64, 8
T = B * S
NT = T // 128
HG = 4
NG = B * H // HG
NQT = S // 128
NPART = 3
ROWS_QK = NPART * NPART * HD
ROWS_BIAS = 2 * NQT * NPART
ROW_MAX = ROWS_QK + ROWS_BIAS
BETA = 48.0
STEPS = 2 * NQT
LAG = 2
NP_SLOTS = 4
TILES = NQT * HG
PARTS_OUT = (16 * 2 * NPART, 16 * NPART)
LOADS = 5
EPS = 1e-5
TAKEN = -3.0e38


def host_constants():
    bf16 = mybir.dt.np(mybir.dt.bfloat16)

    def parts(v):
        out, rest = [], v.astype(np.float32)
        for _ in range(NPART):
            p = rest.astype(bf16)
            out.append(p)
            rest = rest - p.astype(np.float32)
        return out

    slopes = np.power(2.0, 8.0 * np.arange(0, -H, -1) / H).astype(np.float32)
    pos = np.arange(S)
    k_rows = np.zeros((H // HG, 128 - ROWS_QK, HG, S), bf16)
    q_rows = np.zeros((128 - ROWS_QK, HG, S), bf16)
    for j in range(NQT):
        side = np.sign(j - pos // 128).astype(np.float32)
        here = (pos // 128 == j).astype(np.float32)
        for c in range(NPART):
            q_rows[NPART * j + c] = here
            q_rows[NPART * (NQT + j) + c] = here * (pos - 128 * j)
        for h in range(H):
            s = slopes[h]
            line = np.where(side == 0, -BETA * s, side * s * (pos - 128 * j).astype(np.float32)).astype(np.float32)
            for c, (a, b) in enumerate(zip(parts(line), parts(-side * s))):
                k_rows[h // HG, NPART * j + c, h % HG] = a
                k_rows[h // HG, NPART * (NQT + j) + c, h % HG] = b
    k_rows[:, ROWS_BIAS:ROWS_BIAS + NPART] = 1.0
    dist = np.abs(np.arange(128)[:, None] - np.arange(128)[None, :])
    corr = slopes[:, None, None].astype(np.float64) * (BETA - dist)
    select = np.zeros((E // 2, 128, 128), np.float16)
    for e in range(E):
        select[e // 2, e, 64 * (e % 2):64 * (e % 2) + 64] = 1.0
        select[e // 2, E + e, 64 * (e % 2):64 * (e % 2) + 64] = 2.0 ** -12
    return {
        "k_rows": k_rows.reshape(H // HG, 128 - ROWS_QK, HG * S),
        "q_rows": q_rows.reshape(128 - ROWS_QK, HG, 2, S // 2).transpose(0, 2, 1, 3).reshape(-1, HG * S),
        "corr_add": corr.astype(np.float32),
        "corr_mul": np.ascontiguousarray(np.exp(corr).astype(np.float32).transpose(1, 0, 2)),
        "select": select,
        "ident32": np.eye(128, dtype=np.float32),
        "ident16": np.eye(128).astype(bf16),
        "identh": np.eye(128, dtype=np.float16),
    }


def build(nc, a, out):
    f32, bf16, f16, f32r = mybir.dt.float32, mybir.dt.bfloat16, mybir.dt.float16, mybir.dt.float32r
    ALU, ACT, AX = mybir.AluOpType, mybir.ActivationFunctionType, mybir.AxisListType
    ds = bass.ds
    ctx = ExitStack()
    with ctx:
        def sb(name, shape, dt=f32):
            return ctx.enter_context(nc.sbuf_tensor(name, shape, dt))

        def ps(name, shape, dt=f32):
            return ctx.enter_context(nc.psum_tensor(name, shape, dt))

        def sem(name):
            return ctx.enter_context(nc.semaphore(name))

        q_parts = nc.dram_tensor("q_parts", [NPART, NG, HD, HG * S], bf16)
        k_parts = nc.dram_tensor("k_parts", [NG, NPART, HD, HG * S], bf16)

        attn = sb("attn", [128, B, 2, 4, D])
        x1 = sb("x1", [128, NT, D])
        ident32 = sb("ident32_sb", [128, 128])
        ident16 = sb("ident16_sb", [128, 128], bf16)
        identh = sb("identh_sb", [128, 128], f16)
        w_out = sb("w_out", [128, D])
        a_t = sb("a_t", [128, 2, 512])
        stats = sb("stats", [128, NT, 6])
        mean_var = sb("mean_var", [128, NT, 2])
        b_out = sb("b_out", [128, D])
        cent = sb("cent", [128, 2 * E])
        e_bias = sb("e_bias", [2 * E, 1])

        early = ExitStack()

        def sb1(name, shape, dt=f32):
            return early.enter_context(nc.sbuf_tensor(name, shape, dt))

        q_stack = sb1("q_stack", [128, 3, HG * S], bf16)
        k_stack = sb1("k_stack", [128, 3, HG * S], bf16)
        probs = sb1("probs", [128, NP_SLOTS, HG, 512])
        v_all = sb1("v_all", [128, NG, NQT, HG * HD])
        v_stage = sb1("v_stage", [128, NQT, HG, 32])
        corr_add = sb1("corr_add_sb", [128, HG, 15 * 128])
        corr_mul = sb1("corr_mul_sb", [128, H, 128])
        junk = sb1("junk", [128, 2, S], bf16)
        u_sb = sb1("u_sb", [128, 2, 512])
        row_max = sb1("row_max", [128, 2, 16])
        max_rest = sb1("max_rest", [128, 16])
        max_parts = sb1("max_parts", [128, 2, NPART, 16], bf16)
        max_rows = sb1("max_rows", [NPART * 16, 2, 128], bf16)
        rden = sb1("rden", [128, 2, 4, HG, 1])
        w_qkv = sb1("w_qkv", [128, 3 * D])
        b_q = sb1("b_q", [128, 2])
        b_qs = sb1("b_qs", [128, 2])
        b_v = sb1("b_v", [128, D])
        part_sb = sb1("part_sb", [128, 3, NPART, S], bf16)
        flat = probs[:, :, :, :].rearrange("p a b c -> p (a b c)")
        x_t = flat[:, 0:T]
        qk32 = flat[:, T:T + 2 * S].rearrange("p (a b) -> p a b", a=2)
        rest = flat[:, T + 2 * S:T + 4 * S].rearrange("p (a b) -> p a b", a=2)
        early.close()

        x_hi = sb("x_hi", [128, T], f32r)
        x_lo = sb("x_lo", [128, T], f32r)
        cw_t = sb("cw_t", [128, T], f16)
        cent_hi = sb("cent_hi", [128, 2 * E], f32r)
        cent_lo = sb("cent_lo", [128, 2 * E], f32r)
        var_eps = sb("var_eps", [128, NT])
        std = sb("std", [128, NT])
        rstd0 = sb("rstd0", [128, NT])
        shift = sb("shift", [128, NT])
        aff_t = sb("aff_t", [128, 2, 512])
        newton = sb("newton", [128, NT])
        newton2 = sb("newton2", [128, NT])
        rstd = sb("rstd", [128, NT])
        top8 = sb("top8", [128, 4, TOPK])
        marked = sb("marked", [128, 4, E])
        sig = sb("sig", [128, 2, 4, E])
        sel_sig = sb("sel_sig", [128, 2, 4, E])
        wsum = sb("wsum", [128, 4])
        wsum_eps = sb("wsum_eps", [128, 4])
        wrec = sb("wrec", [128, 2, 4])
        cw = sb("cw", [128, 2, 4, E])
        cw_rest = sb("cw_rest", [128, 2, 4, E])
        cw_half = sb("cw_half", [128, 2, 4, 2 * E], f16)
        w_raw = sb("w_raw", [128, 2, 256])
        w_hi = sb("w_hi", [128, 2, 256], f32r)
        w_lo = sb("w_lo", [128, 2, 256], f32r)
        w_sel = sb("w_sel", [128, 2, 128], f16)
        ws_raw = sb("ws_raw", [128, 256])
        ws_hi = sb("ws_hi", [128, 256], f32r)
        ws_lo = sb("ws_lo", [128, 256], f32r)
        hid = sb("hid", [128, 2, 512])
        hid_w = sb("hid_w", [128, 2, 512])
        hid_hi = sb("hid_hi", [128, 4, 512], f32r)
        hid_lo = sb("hid_lo", [128, 4, 512], f32r)
        y_t = sb("y_t", [128, 4, 512])

        ring_a = ps("ring_a", [128, 2, S])
        ring_b = ps("ring_b", [128, 2, 512])
        ring_u = ps("ring_u", [128, 2, 512])

        ld_first = sem("ld_first")
        ld_const = sem("ld_const")
        ld_x = [sem(f"ld_x{b}") for b in range(B)]
        ld_res = sem("ld_res")
        zeroed = sem("zeroed")
        qk_full = sem("qk_full")
        qk_taken = sem("qk_taken")
        act_chain = sem("act_chain")
        rest_d = sem("rest_d")
        rest_p = sem("rest_p")
        mid = sem("mid")
        low_d = sem("low_d")
        low_p = sem("low_p")
        parts_out = [sem("q_parts_out"), sem("k_parts_out")]
        v_full = sem("v_full")
        v_taken = sem("v_taken")
        stacked = sem("stacked")
        corr_ld = [sem(f"corr_ld{h}") for h in range(HG)]
        a_full = sem("a_full")
        a_free = sem("a_free")
        dve_chain = sem("dve_chain")
        max_split = sem("max_split")
        max_in = sem("max_in")
        st_full = sem("st_full")
        exp_done = sem("exp_done")
        diag_done = sem("diag_done")
        v_staged = sem("v_staged")
        pv_done = sem("pv_done")
        u_taken = sem("u_taken")
        v_init = sem("v_init")

        res_ready = sem("res_ready")
        at_full = sem("at_full")
        at_sb = sem("at_sb")
        pr_full = sem("pr_full")
        pr_taken = sem("pr_taken")
        var_ready = sem("var_ready")
        std_ready = sem("std_ready")
        rstd_done = sem("rstd_done")
        normed_a = sem("normed_a")
        normed_d = sem("normed_d")
        xt_full = sem("xt_full")
        xt_hi = sem("xt_hi")
        xt_lo = sem("xt_lo")
        cent_split = sem("cent_split")
        afft_full = sem("afft_full")
        aff_sb = sem("aff_sb")
        aff_full = sem("aff_full")
        sig_done = sem("sig_done")
        aff_taken = sem("aff_taken")
        sel_done = sem("sel_done")
        cw_done = sem("cw_done")
        cw_hi_done = sem("cw_hi_done")
        pool_chain = sem("pool_chain")
        cw_split = sem("cw_split")
        cwt_full = sem("cwt_full")
        cwt_sb = sem("cwt_sb")
        w_ld = [sem("w_ld0"), sem("w_ld1")]
        ws_ld = sem("ws_ld")
        w_hi_done = sem("w_hi_done")
        up_split = sem("up_split")
        w_split = sem("w_split")
        ws_split = sem("ws_split")
        h_full = sem("h_full")
        h_act = sem("h_act")
        cb_full = sem("cb_full")
        hw_done = sem("hw_done")
        hi_done = sem("hi_done")
        lo_done = sem("lo_done")
        dn_done = sem("dn_done")
        acc_sb = sem("acc_sb")
        yt_full = sem("yt_full")
        yt_taken = sem("yt_taken")
        out_done = sem("out_done")
        waited_pool = sem("waited_pool")

        block = ctx.enter_context(nc.Block())

        LD_CONST = 12 * 16
        N_CHUNK = NT // 4
        U_HALF = (E // 2 + 1) * 4
        DOWN_LAG = 3

        def ring_step(s, first, last):
            e = []
            if s == 2:
                e.append(("max", 1))
            if s == 3 and not first:
                e.append(("u", 1))
            if s == 10 and not last:
                e.append(("max", 0))
            if s == 11:
                e.append(("u", 0))
            if not last:
                e += [("tile", 2 * s), ("tile", 2 * s + 1)]
            elif 4 <= s < 11:
                e += [("at", c) for c in [s - 4] if c < 6] + [("pr", c) for c in [s - 5] if c >= 0]
            elif s == 12:
                e.append(("at", 6))
            elif s == 13:
                e.append(("pr", 6))
            return e

        def ring_list(first, last):
            return [x for s in range(STEPS) for x in ring_step(s, first, last)]

        FULL = len(ring_list(False, False))
        START = TILES + 1
        MAX_AT = 20

        def ring_base(i, first):
            return START if first else START - 1 + i * FULL

        def base_slot(first):
            return (START if first else START - 1) % 2

        def entry_of(kind, first, last):
            return ring_list(first, last).index(kind)

        LAST_ENTRY = START - 1 + (NG - 1) * FULL + len(ring_list(False, True)) + 1

        def tile_of(k):
            u, r = divmod(k, TILES // 2)
            return 4 * u + r % 4, r // 4

        def q_at(u, h, pos):
            return (u * HG + h) * 512 + pos

        def diag_index(s):
            qh, kt = divmod(s, NQT)
            return None if kt // 4 != qh else (s if qh == 0 else s - 8)

        acc = ring_a[:, :, :].rearrange("p a (b n) -> p (a b) n", b=2)

        @block.sync
        def _(sp):
            for dst, src in ((w_qkv[:, :], a["w_qkv_t"]), (b_q[:, :], a["b_qk"])):
                sp.dma_start(dst, src).then_inc(ld_first, 16)
            for b in range(B):
                sp.dma_start(x_t[:, b * S:b * S + S], a["x_t"][:, b * S:b * S + S]).then_inc(ld_x[b], 16)
            for buf in range(3):
                sp.dma_start(q_stack[ROWS_QK:128, buf, :], a["q_rows"]).then_inc(ld_const, 16)
            for dst, src in ((ident32[:, :], a["ident32"]), (ident16[:, :], a["ident16"]), (identh[:, :], a["identh"]),
                             (corr_mul[:, :, :], a["corr_mul"]), (b_v[:, :], a["b_v"].to_broadcast([128, D])),
                             (w_out[:, :], a["w_out_t"]), (b_out[:, :], a["b_out"].to_broadcast([128, D])),
                             (cent[:, :], a["cent_t"]), (e_bias[:, :], a["e_bias"])):
                sp.dma_start(dst, src).then_inc(ld_const, 16)

            def parts_to_dram(j, parts=range(NPART)):
                b, isk = divmod(j, 2)
                if isk:
                    for c in parts:
                        sp.dma_start(k_parts[4 * b:4 * b + 4, c, :, :].rearrange("g d (h s) -> g (d h) s", h=HG),
                                     part_sb[:, j % 3, c, :]).then_inc(parts_out[1], 16)
                else:
                    for c in parts:
                        for u in range(2):
                            sp.dma_start(q_parts[c, 4 * b:4 * b + 4, :, 2048 * u:2048 * u + 2048].rearrange(
                                "g d (h s) -> (g d) h s", h=HG), part_sb[:, j % 3, c, 512 * u:512 * u + 512]
                            ).then_inc(parts_out[0], 16)

            def load_bias(n):
                sp.dma_start(k_stack[ROWS_QK:128, ds(n % 3, 1), :].rearrange("p a s -> p (a s)"),
                             a["k_rows"][ds(n % 4, 1), :, :].rearrange("a p s -> p (a s)")).then_inc(stacked, 16)

            load_bias(0)
            for c, made in enumerate((qk_taken, mid, low_d)):
                for j in range(2):
                    sp.wait_ge(made, j + 1)
                    parts_to_dram(j, [c])
            for isk in range(2):
                sp.wait_ge(parts_out[isk], PARTS_OUT[isk])

            def load_stack(n):
                buf = n % 3
                sp.dma_start(k_stack[0:ROWS_QK, ds(buf, 1), :].rearrange("p a s -> p (a s)"),
                             k_parts[ds(n, 1), :, :, :].rearrange("a c d s -> a (c d) s")
                             .to_broadcast([NPART, NPART * HD, HG * S])).then_inc(stacked, 16)
                for i in range(NPART):
                    r = NPART * HD * i
                    sp.dma_start(q_stack[r:r + NPART * HD, ds(buf, 1), :].rearrange("p a s -> p (a s)"),
                                 q_parts[i:i + 1, ds(n, 1), :, :].rearrange("c a d s -> (c a) d s")
                                 .to_broadcast([NPART, HD, HG * S])).then_inc(stacked, 16)

            def load_corr(n, h):
                sp.dma_start(corr_add[:, h, 7 * 128:8 * 128],
                             a["corr_add"][ds((n % 4) * HG + h, 1), :, :].rearrange("a p k -> p (a k)")
                             ).then_inc(corr_ld[h], 16)

            def max_rows_in(n, u):
                buf = n % 3
                sp.dma_start(q_stack[ROW_MAX:ROW_MAX + NPART, ds(buf, 1), 2048 * u:2048 * u + 2048]
                             .rearrange("p a s -> p (a s)"), max_rows[:, u, :]).then_inc(max_in, 16)

            load_stack(0)
            sp.wait_ge(zeroed, 1)
            for h in range(HG):
                load_corr(0, h)
            sp.wait_ge(stacked, 16 * LOADS)
            load_bias(1)
            load_stack(1)
            for j in range(2, 2 * B):
                if j == 2 * B - 2:
                    sp.wait_ge(a_free, MAX_AT + 1)
                    max_rows_in(0, 0)
                if j >= 2 * B - 2:
                    h = j - (2 * B - 2)
                    sp.wait_ge(a_free, 21 + 4 * h)
                    load_corr(1, h)
                sp.wait_ge(low_p, j - 1)
                sp.wait_ge(parts_out[j % 2], PARTS_OUT[j % 2] * (j // 2))
                parts_to_dram(j)
            sp.wait_ge(a_free, 21 + 4 * 2)
            load_corr(1, 2)
            for c in range(N_CHUNK):
                sp.dma_start(x1[:, 4 * c:4 * c + 4, :],
                             a["x"][512 * c:512 * c + 512, :].rearrange("(t p) d -> p t d", p=128)
                             ).then_inc(ld_res, 16)
            for isk in range(2):
                sp.wait_ge(parts_out[isk], PARTS_OUT[isk] * B)

            def iteration(i, first, last, load):
                base = ring_base(i, first)
                sp.wait_ge(a_free, base + entry_of(("max", 1), first, last) + 1)
                sp.wait_ge(max_in, (2 * i + 1) * 16)
                max_rows_in(i, 1)
                if not last:
                    load_corr(i + 1, HG - 1)
                if load:
                    if not first:
                        sp.wait_ge(st_full, i * STEPS * HG)
                    sp.wait_ge(stacked, (i + 2) * 16 * LOADS)
                    load_bias(i + 2)
                    load_stack(i + 2)
                if not last:
                    for h in range(HG - 1):
                        if load:
                            sp.wait_ge(a_free, base + entry_of(("tile", 19 + 4 * h), first, last) + 1)
                            load_corr(i + 2, h)
                        if h == 0:
                            sp.wait_ge(a_free, base + entry_of(("max", 0), first, last) + 1)
                            sp.wait_ge(max_in, (2 * i + 2) * 16)
                            max_rows_in(i + 1, 0)

            iteration(0, True, False, True)
            with sp.Fori(1, NG - 2) as i:
                iteration(i, False, False, True)
            iteration(NG - 2, False, False, False)
            iteration(NG - 1, False, True, False)

            sp.wait_ge(a_free, LAST_ENTRY)
            sp.dma_start(ws_raw[:, :], a["w_shared"]).then_inc(ws_ld, 16)

            def load_pair(half, pair, par, first):
                if not first:
                    sp.wait_ge(w_split, half * (E // 2) + pair - 1)
                    sp.wait_ge(cb_full, (half * (E // 2) + pair - 1) * 4)
                sp.dma_start(w_raw[:, par, :], a["w_pairs"][ds(pair, 1), :, :].rearrange("a p n -> p (a n)")
                             ).then_inc(w_ld[par], 16)
                sp.dma_start(w_sel[:, par, :], a["select"][ds(pair, 1), :, :].rearrange("a p n -> p (a n)")
                             ).then_inc(w_ld[par], 16)

            for half in range(2):
                load_pair(half, 0, 0, half == 0)
                load_pair(half, 1, 1, half == 0)
                with sp.Fori(1, E // 4) as j:
                    for par in range(2):
                        load_pair(half, 2 * j + par, par, False)
            for c in range(N_CHUNK):
                sp.wait_ge(normed_a, N_CHUNK + c + 1)
                sp.wait_ge(normed_d, N_CHUNK + c + 1)
                sp.dma_start(out[512 * c:512 * c + 512, :].rearrange("(t p) d -> p t d", p=128),
                             x1[:, 4 * c:4 * c + 4, :]).then_inc(out_done, 16)
            sp.wait_ge(out_done, 16 * N_CHUNK)

        @block.tensor
        def _(pe):
            def project_qk(j):
                b, isk = divmod(j, 2)
                if j < 2:
                    psum = ring_a[:, j, :]
                else:
                    psum = ring_b[:, :, :].rearrange("p a b -> p (a b)")
                    if j > 2:
                        pe.wait_ge(qk_taken, j)
                pe.wait_ge(ld_x[b], 16)
                for n in range(2):
                    last = nc.tensor.matmul(psum[:, 512 * n:512 * n + 512], w_qkv[:, D * isk:D * isk + D],
                                            x_t[:, b * S + 512 * n:b * S + 512 * n + 512], start=True, stop=True)
                last.then_inc(qk_full, 1)

            def project_v(j):
                if j >= 2:
                    pe.wait_ge(v_taken, j - 1)
                pe.wait_ge(ld_x[j // 2], 16)
                for t in range(4):
                    last = nc.tensor.matmul(ring_u[:, j % 2, D * t:D * t + D],
                                            x_t[:, (4 * j + t) * 128:(4 * j + t + 1) * 128],
                                            w_qkv[:, 2 * D:3 * D], start=True, stop=True)
                last.then_inc(v_full, 1)

            pe.wait_ge(ld_first, 32)
            project_qk(0)
            project_qk(1)
            project_v(0)
            project_v(1)

            def tile_half(n, k, slot, half):
                qt, h = tile_of(k)
                buf = n % 3
                return nc.tensor.matmul(
                    ring_a[:, slot, 512 * half:512 * half + 512],
                    q_stack[0:ROW_MAX, ds(buf, 1), q_at(qt // 4, h, 128 * (qt % 4)):q_at(qt // 4, h, 128 * (qt % 4)) + 128]
                    .rearrange("p a s -> p (a s)"),
                    k_stack[0:ROW_MAX, ds(buf, 1), h * S + 512 * half:h * S + 512 * half + 512].rearrange("p a s -> p (a s)"),
                    start=True, stop=True)

            def transpose_attn(c, psum):
                for t in range(4):
                    last = nc.tensor.transpose(psum[:, 128 * t:128 * t + 128], attn[:, c // 2, c % 2, t, :],
                                               ident32[:, :])
                return last

            def project_out(c, psum):
                for t in range(4):
                    last = nc.tensor.matmul(psum[:, 128 * t:128 * t + 128], a_t[:, c % 2, 128 * t:128 * t + 128],
                                            w_out[:, :], start=True, stop=True)
                return last

            def units(n_tile, i, entry, kind, x, slot, first):
                def free():
                    pe.wait_ge(a_free, entry - 1)
                if kind == "tile":
                    def one():
                        free()
                        tile_half(n_tile, x, slot, 0)
                    return [one, lambda: tile_half(n_tile, x, slot, 1).then_inc(a_full, 1)]
                if kind == "max":
                    def one():
                        free()
                        g = i if x == 1 else i + 1
                        pe.wait_ge(max_split, 2 * g + x + 1)
                        nc.tensor.transpose(ring_a[0:NPART * 16, slot, 0:64].bitcast(bf16),
                                            max_parts[:, x, :, :].rearrange("p c n -> p (c n)"),
                                            ident16[:, :]).then_inc(a_full, 1)
                    return [one]
                if kind == "at":
                    def one():
                        pe.wait_ge(a_free, entry)
                        transpose_attn(x, ring_a[:, slot, 0:512]).then_inc(a_full, 1)
                    return [one]
                if kind == "pr":
                    def one():
                        pe.wait_ge(a_free, ring_base(i, first) + entry_of(("at", x), first, True) + 1)
                        project_out(x, ring_a[:, slot, 0:512]).then_inc(a_full, 1)
                    return [one]

                def one():
                    free()
                    pe.wait_ge(u_taken, 2 * i + 1 - x)
                    for t in range(4):
                        last = nc.tensor.transpose(ring_a[:, slot, 128 * t:128 * t + 128],
                                                   u_sb[:, x, 128 * t:128 * t + 128], ident32[:, :])
                    last.then_inc(a_full, 1)
                return [one]

            def p_t_v(i, s, h):
                qh, kt = divmod(s, NQT)
                if h == 0:
                    if kt == 0:
                        if not isinstance(i, int) or 2 * i + qh >= 2:
                            pe.wait_ge(u_taken, 2 * i + qh - 1)
                    if s in (0, 4):
                        pe.wait_ge(v_staged, 2 * i + s // 4 + 1)
                    if diag_index(s) is not None:
                        pe.wait_ge(diag_done, 8 * i + diag_index(s) + 1)
                if diag_index(s) is None:
                    pe.wait_ge(exp_done, (STEPS * i + s) * HG + h + 1)
                last = nc.tensor.matmul(ring_u[32 * h:32 * h + 32, qh, :], v_stage[:, kt, h, :],
                                        probs[:, s % NP_SLOTS, h, :], start=kt == 0, stop=kt == NQT - 1)
                if h == HG - 1:
                    last.then_inc(pv_done, 1)

            pe.wait_ge(stacked, 16 * LOADS)
            pe.wait_ge(qk_taken, 2)
            others = [lambda j=j: project_qk(j) for j in range(2, 2 * B)]
            for n, j in enumerate(range(2, 2 * B)):
                others.insert(2 * n + 1, lambda j=j: project_v(j))
            for k in range(TILES):
                if k == MAX_AT:
                    units(0, -1, MAX_AT, "max", 0, MAX_AT % 2, True)[0]()
                entry = k + (k >= MAX_AT)
                if k >= 2:
                    pe.wait_ge(a_free, entry - 1)
                tile_half(0, k, entry % 2, 0)
                tile_half(0, k, entry % 2, 1).then_inc(a_full, 1)
                if k % 2 and others:
                    others.pop(0)()
            pe.wait_ge(qk_taken, 2 * B)
            pe.wait_ge(v_taken, 2 * B)

            def iteration(i, first, last):
                base, entry = ring_base(i, first), 0
                if not last:
                    pe.wait_ge(stacked, (i + 2) * 16 * LOADS)
                buf = i % 3
                for s in range(STEPS):
                    qh, kt = divmod(s, NQT)
                    work = []
                    for kind, x in ring_step(s, first, last):
                        work += units(i + 1, i, base + entry, kind, x, (base_slot(first) + entry) % 2, first)
                        entry += 1
                    if kt == 0:
                        pe.wait_ge(max_in, (2 * i + qh + 1) * 16)

                    def scores(h):
                        n = s * HG + h
                        if not (first and n < 2):
                            pe.wait_ge(exp_done, i * STEPS * HG + n - 1)
                        nc.tensor.matmul(
                            ring_b[:, h % 2, :],
                            k_stack[:, ds(buf, 1), h * S + 128 * kt:h * S + 128 * kt + 128].rearrange("p a s -> p (a s)"),
                            q_stack[:, ds(buf, 1), q_at(qh, h, 0):q_at(qh, h, 0) + 512].rearrange("p a s -> p (a s)"),
                            start=True, stop=True).then_inc(st_full, 1)

                    scores(0)
                    scores(1)
                    for h in range(HG):
                        if s >= LAG:
                            p_t_v(i, s - LAG, h)
                        elif not first:
                            p_t_v(i - 1, s - LAG + STEPS, h)
                    scores(2)
                    scores(3)
                    for call in work:
                        call()

            iteration(0, True, False)
            for i in range(1, NG - 1):
                iteration(i, False, False)
            iteration(NG - 1, False, True)
            for s in range(STEPS - LAG, STEPS):
                for h in range(HG):
                    p_t_v(NG - 1, s, h)
            units(0, NG, LAST_ENTRY - 1, "u", 1, (LAST_ENTRY - 1) % 2, False)[0]()

            for c in range(N_CHUNK + 4):
                if c < N_CHUNK:
                    pe.wait_ge(normed_a, c + 1)
                    pe.wait_ge(normed_d, c + 1)
                    if c >= 2:
                        pe.wait_ge(xt_lo, c - 1)
                    for t in range(4):
                        last = nc.tensor.transpose(ring_b[:, c % 2, 128 * t:128 * t + 128], x1[:, 4 * c + t, :],
                                                   ident32[:, :])
                    last.then_inc(xt_full, 1)
                if c == 0:
                    pe.wait_ge(a_free, LAST_ENTRY)
                    transpose_attn(N_CHUNK - 1, ring_u[:, 0, :]).then_inc(at_full, 1)
                n = c - 1
                if 0 <= n < N_CHUNK:
                    if n == 0:
                        pe.wait_ge(cent_split, 2)
                    pe.wait_ge(xt_lo, n + 1)
                    if n >= 2:
                        pe.wait_ge(aff_sb, n - 1)
                    tok = slice(512 * n, 512 * n + 512)
                    for m, (w, x) in enumerate(((cent_hi, x_hi), (cent_lo, x_hi), (cent_hi, x_lo))):
                        last = nc.tensor.matmul(ring_a[:, n % 2, 512:1024], w[:, :], x[:, tok], start=m == 0, stop=m == 2)
                    last.then_inc(afft_full, 1)
                if c == 1:
                    pe.wait_ge(at_sb, 1)
                    project_out(N_CHUNK - 1, ring_u[:, 1, :]).then_inc(pr_full, 1)
                n = c - 2
                if 0 <= n < N_CHUNK:
                    pe.wait_ge(aff_sb, n + 1)
                    if n == 1:
                        pe.wait_ge(pr_taken, 1)
                    if n >= 2:
                        pe.wait_ge(aff_taken, n - 1)
                    for t in range(4):
                        last = nc.tensor.transpose(ring_u[:, n % 2, 128 * t:128 * t + 128],
                                                   aff_t[:, n % 2, 128 * t:128 * t + 128], ident32[:, :])
                    last.then_inc(aff_full, 1)
                n = c - 4
                if n >= 0:
                    pe.wait_ge(cw_split, n + 1)
                    if n >= 2:
                        pe.wait_ge(cwt_sb, n - 1)
                    for t in range(4):
                        last = nc.tensor.transpose(ring_a[:, n % 2, 64 * t:64 * t + 64].bitcast(f16),
                                                   cw_half[:, n % 2, t, :], identh[:, :])
                    last.then_inc(cwt_full, 1)
            pe.wait_ge(cwt_sb, N_CHUNK)

            def up(half, pair, par, q, skip):
                p = E // 2 if pair is None else pair
                unit = half * U_HALF + p * 4 + q
                hi, lo = (ws_hi[:, 0:128], ws_lo[:, 0:128]) if pair is None else (w_hi[:, par, 0:128], w_lo[:, par, 0:128])
                if q == 0:
                    if pair is None:
                        pe.wait_ge(ws_split, 2)
                    else:
                        pe.wait_ge(up_split, half * (E // 2) + pair + 1)
                if not skip:
                    pe.wait_ge(hw_done, unit - 1)
                tok = half * (T // 2) + 512 * q
                for m, (w, x) in enumerate(((hi, x_hi), (hi, x_lo), (lo, x_hi))):
                    last = nc.tensor.matmul(ring_b[:, q % 2, :], w, x[:, tok:tok + 512], start=m == 0, stop=m == 2)
                last.then_inc(h_full, 1)
                if pair is not None:
                    nc.tensor.matmul(ring_u[:, q % 2, :], w_sel[:, par, :], cw_t[:, tok:tok + 512],
                                     start=True, stop=True).then_inc(cb_full, 1)

            def finish(half, q):
                pe.wait_ge(acc_sb, 4 * half + q + 1)
                for t in range(4):
                    last = nc.tensor.transpose(acc[:, q, 128 * t:128 * t + 128],
                                               y_t[:, q, 128 * t:128 * t + 128], ident32[:, :])
                last.then_inc(yt_full, 1)

            def down(half, pair, par, q, start=False, stop=False):
                p = E // 2 if pair is None else pair
                unit = half * U_HALF + p * 4 + q
                hi, lo = (ws_hi[:, 128:256], ws_lo[:, 128:256]) if pair is None else (
                    w_hi[:, par, 128:256], w_lo[:, par, 128:256])
                if q == 0 and pair is not None:
                    pe.wait_ge(w_split, half * (E // 2) + pair + 1)
                if half and start:
                    pe.wait_ge(yt_taken, q + 1)
                pe.wait_ge(lo_done, unit + 1)
                for m, (w, h) in enumerate(((hi, hid_hi), (lo, hid_hi), (hi, hid_lo))):
                    last = nc.tensor.matmul(acc[:, q, :], w, h[:, q, :], start=start and m == 0, stop=stop and m == 2)
                last.then_inc(dn_done, 1)

            def pairs(half, j, first):
                for u in range(8):
                    if half and first and u < 4:
                        finish(0, u)
                    up(half, 2 * j + u // 4, u // 4, u % 4, first and half == 0 and u < 2)
                    if u >= DOWN_LAG:
                        d = u - DOWN_LAG
                        down(half, 2 * j + d // 4, d // 4, d % 4, start=first and d < 4)
                    elif not first:
                        down(half, 2 * j - 1, 1, u - DOWN_LAG + 4)

            for half in range(2):
                pairs(half, 0, True)
                with pe.Fori(1, E // 4) as j:
                    pairs(half, j, False)
                for q in range(4):
                    up(half, None, 0, q, False)
                    if q < DOWN_LAG:
                        down(half, E // 2 - 1, 1, q - DOWN_LAG + 4)
                    else:
                        down(half, None, 0, q - DOWN_LAG, stop=True)
                for q in range(4 - DOWN_LAG, 4):
                    down(half, None, 0, q, stop=True)
            for q in range(4):
                finish(1, q)

        @block.scalar
        def _(act):
            scale = 1.0 / float(np.sqrt(HD))
            act.wait_ge(ld_first, 32)
            nc.scalar.mul(b_qs[:, 0:1], b_q[:, 0:1], scale).then_inc(act_chain, 1)
            nc.scalar.copy(b_qs[:, 1:2], b_q[:, 1:2]).then_inc(act_chain, 1)
            act.wait_ge(act_chain, 2)

            def take_qk(j):
                isk = j % 2
                act.wait_ge(qk_full, j + 1)
                if j >= 2:
                    if j < 4:
                        act.wait_ge(rest_d, j - 1)
                    else:
                        act.wait_ge(rest_p, j - 3)
                if j >= 3:
                    act.wait_ge(parts_out[1 - isk], PARTS_OUT[1 - isk] * ((j - 3) // 2 + 1))
                psum = ring_a[:, j, :] if j < 2 else ring_b[:, :, :].rearrange("p a b -> p (a b)")
                nc.scalar.activation(qk32[:, j % 2, :], psum, ACT.Identity,
                                     bias=b_qs[:, isk:isk + 1], scale=1.0 if isk else scale).then_inc(act_chain, 1)
                act.wait_ge(act_chain, 3 + j)
                nc.scalar.copy(part_sb[:, j % 3, 0, :], qk32[:, j % 2, :]).then_inc(qk_taken, 1)

            def middle_part(j):
                if j < 2:
                    act.wait_ge(rest_d, j + 1)
                else:
                    act.wait_ge(rest_p, j - 1)
                nc.scalar.copy(part_sb[:, j % 3, 1, :], rest[:, j % 2, :]).then_inc(mid, 1)

            def take_v(j):
                b, half = divmod(j, 2)
                act.wait_ge(v_full, j + 1)
                nc.scalar.copy(v_all[:, 4 * b:4 * b + 4, 4 * half:4 * half + 4, :].rearrange("p g t c -> p t g c"),
                               ring_u[:, j % 2, :].rearrange("p (t g c) -> p t g c", t=4, g=4)).then_inc(v_taken, 1)

            take_qk(0)
            take_qk(1)
            middle_part(0)
            middle_part(1)
            take_v(0)
            take_v(1)
            for j in range(2, 2 * B):
                take_qk(j)
                take_v(j)
                middle_part(j)

            def take_u(i, qh, done=False):
                act.wait_ge(pv_done, STEPS * i + NQT * (qh + 1))
                if not isinstance(i, int) or i > 0:
                    act.wait_ge(a_full, START - 1 + FULL * (i - 1 + qh) + entry_of(("u", qh), False, done) + 1)
                nc.scalar.copy(u_sb[:, qh, :], ring_u[:, qh, :]).then_inc(u_taken, 1)

            def iteration(i, first, last):
                for s in range(STEPS):
                    for h in range(HG):
                        n = s * HG + h
                        act.wait_ge(st_full, i * STEPS * HG + n + 1)
                        if h == 0 and not (first and s < NP_SLOTS):
                            act.wait_ge(pv_done, STEPS * i + s - NP_SLOTS + 1)
                        nc.scalar.activation(probs[:, s % NP_SLOTS, h, :], ring_b[:, h % 2, :], ACT.Exp
                                             ).then_inc(exp_done, 1)
                    if s == 2 and not first:
                        take_u(i - 1, 1)
                    if s == 10:
                        take_u(i, 0)

            act.wait_ge(low_p, 2 * B - 2)
            iteration(0, True, False)
            for i in range(1, NG - 1):
                iteration(i, False, False)
            iteration(NG - 1, False, True)

            def std_dev(n, tiles):
                act.wait_ge(var_ready, n + 1)
                nc.scalar.activation(std[:, tiles], var_eps[:, tiles], ACT.Sqrt).then_inc(std_ready, 1)

            std_dev(0, slice(0, NT - 4))
            take_u(NG - 1, 1, True)
            def norm(c):
                for t in range(4 * c, 4 * c + 2):
                    last = nc.scalar.activation(x1[:, t, :], x1[:, t, :], ACT.Identity,
                                                bias=shift[:, t:t + 1], scale=rstd[:, t:t + 1])
                last.then_inc(normed_a, 1)

            act.wait_ge(rstd_done, 1)
            norm(0)
            for c in range(N_CHUNK + 4):
                if c + 1 < N_CHUNK:
                    if c + 1 == N_CHUNK - 1:
                        act.wait_ge(rstd_done, 2)
                    norm(c + 1)
                if c < N_CHUNK:
                    act.wait_ge(xt_full, c + 1)
                    nc.scalar.copy(x_hi[:, 512 * c:512 * c + 512], ring_b[:, c % 2, :]).then_inc(xt_hi, 1)
                if c == 0:
                    act.wait_ge(at_full, 1)
                    nc.scalar.copy(a_t[:, (N_CHUNK - 1) % 2, :], ring_u[:, 0, :]).then_inc(at_sb, 1)
                n = c - 1
                if 0 <= n < N_CHUNK:
                    act.wait_ge(afft_full, n + 1)
                    if n >= 2:
                        act.wait_ge(aff_full, n - 1)
                    nc.scalar.activation(aff_t[:, n % 2, :], ring_a[:, n % 2, 512:1024], ACT.Identity,
                                         bias=e_bias[:, 0:1], scale=1.0).then_inc(aff_sb, 1)
                if c == 1:
                    std_dev(1, slice(NT - 4, NT))
                n = c - 2
                if 0 <= n < N_CHUNK:
                    act.wait_ge(aff_full, n + 1)
                    if n >= 2:
                        act.wait_ge(sel_done, n - 1)
                    nc.scalar.activation(sig[:, n % 2, :, :],
                                         ring_u[:, n % 2, :].rearrange("p (t e) -> p t e", t=4)[:, :, 0:E],
                                         ACT.Sigmoid).then_inc(sig_done, 1)
                n = c - 3
                if 0 <= n < N_CHUNK:
                    act.wait_ge(cw_done, n + 1)
                    if n >= 2:
                        act.wait_ge(cwt_full, n - 1)
                    nc.scalar.copy(cw_half[:, n % 2, :, 0:E], cw[:, n % 2, :, :]).then_inc(cw_hi_done, 1)
                n = c - 4
                if n >= 0:
                    act.wait_ge(cwt_full, n + 1)
                    nc.scalar.copy(cw_t[:, 512 * n:512 * n + 512], ring_a[:, n % 2, 0:256].bitcast(f16)
                                   ).then_inc(cwt_sb, 1)

            def gate(unit, q):
                act.wait_ge(h_full, unit + 1)
                nc.scalar.activation(hid[:, q % 2, :], ring_b[:, q % 2, :], ACT.Silu).then_inc(h_act, 1)

            def high(unit, q, skip):
                act.wait_ge(hw_done, unit + 1)
                if not skip:
                    act.wait_ge(dn_done, unit - 3)
                nc.scalar.copy(hid_hi[:, q, :], hid_w[:, q % 2, :]).then_inc(hi_done, 1)

            def units(half, base, n, first, second=False):
                for u in range(n):
                    if second and u >= 4:
                        if u == 4:
                            act.wait_ge(rstd_done, 3)
                        norm(u - 4)
                    gate(base + u, u % 4)
                    if not (first and u == 0):
                        high(base + u - 1, (u - 1) % 4, first and half == 0 and u < 5)

            def take_acc(half, q):
                act.wait_ge(dn_done, (half + 1) * U_HALF - 3 + q)
                if half:
                    act.wait_ge(yt_full, q + 1)
                nc.scalar.copy(y_t[:, q, :], acc[:, q, :]).then_inc(acc_sb, 1)

            for half in range(2):
                if half:
                    for q in range(4):
                        take_acc(0, q)
                units(half, half * U_HALF, 8, True)
                if half:
                    std_dev(2, slice(0, 16))
                    units(half, U_HALF + 8, 8, False, True)
                with act.Fori(1 + half, E // 4) as j:
                    units(half, half * U_HALF + 8 * j, 8, False)
                units(half, half * U_HALF + 2 * E, 4, False)
                high((half + 1) * U_HALF - 1, 3, False)
            for q in range(4):
                take_acc(1, q)
            std_dev(3, slice(16, 32))
            act.wait_ge(rstd_done, 4)
            for c in range(4, 8):
                norm(c)

        @block.vector
        def _(dve):
            for j in range(2):
                dve.wait_ge(qk_taken, j + 1)
                nc.vector.tensor_tensor(rest[:, j, :], qk32[:, j, :], part_sb[:, j, 0, :],
                                        ALU.subtract).then_inc(rest_d, 1)
            for j in range(2):
                dve.wait_ge(mid, j + 1)
                nc.vector.tensor_tensor(part_sb[:, j, 2, :], rest[:, j, :], part_sb[:, j, 1, :],
                                        ALU.subtract).then_inc(low_d, 1)

            def pass_a_tile(n, k, slot, entry):
                qt, h = tile_of(k)
                if k % 16 % 4 == 0:
                    dve.wait_ge(corr_ld[h], 16 * (n + 1))
                dve.wait_ge(a_full, entry + 1)
                u = qt // 4
                col = 4 * h + qt % 4
                nc.vector.tensor_tensor_reduce(
                    out=junk[:, slot, :], in0=ring_a[:, slot, :],
                    in1=corr_add[:, h, 896 - 128 * qt:896 - 128 * qt + S],
                    scale=1.0, scalar=-3.0e38, op0=ALU.add, op1=ALU.max,
                    accum_out=row_max[:, u, col:col + 1]).then_inc(a_free, 1)

            steps = [0]

            def link(ins, wait=True):
                steps[0] += 1
                ins.then_inc(dve_chain, 1)
                if wait:
                    dve.wait_ge(dve_chain, steps[0])

            def split_max(u, step, entries=None):
                if step == 0:
                    dve.wait_ge(a_free, entries)
                    link(nc.vector.tensor_scalar(max_parts[:, u, 0, :], row_max[:, u, :], -1.0, None, ALU.mult), False)
                    return
                dve.wait_ge(dve_chain, steps[0])
                if step == 1:
                    link(nc.vector.scalar_tensor_tensor(max_rest[:, :], row_max[:, u, :], -1.0, max_parts[:, u, 0, :],
                                                        ALU.mult, ALU.subtract), False)
                elif step == 2:
                    link(nc.vector.tensor_copy(max_parts[:, u, 1, :], max_rest[:, :]), False)
                else:
                    nc.vector.tensor_tensor(max_parts[:, u, 2, :], max_rest[:, :], max_parts[:, u, 1, :],
                                            ALU.subtract).then_inc(max_split, 1)

            def take_max(n, u, slot, entry, wait):
                dve.wait_ge(a_full, entry + 1)
                if wait:
                    dve.wait_ge(max_in, (2 * n + u - 1) * 16)
                nc.vector.tensor_copy(max_rows[:, u, :], ring_a[0:NPART * 16, slot, 0:64].bitcast(bf16)
                                      ).then_inc(a_free, 1)

            def take_out(n, u, slot, entry):
                dve.wait_ge(a_full, entry + 1)
                v = ring_a[:, slot, 0:512].rearrange("p (t h c) -> p t h c", t=4, h=HG)
                link(nc.vector.reciprocal(rden[:, u, :, :, :], v[:, :, :, HD:HD + 1]))
                nc.vector.tensor_tensor(
                    attn[:, ds(n // (H // HG), 1), u, :, ds((n % (H // HG)) * HG * HD, HG * HD)]
                    .rearrange("p a t (h c) -> p (a t) h c", h=HG),
                    v[:, :, :, 0:HD], rden[:, u, :, :, :].to_broadcast([128, 4, HG, HD]), ALU.mult
                ).then_inc(a_free, 1)

            def add_rows(c, psum):
                rows = x1[:, 4 * c:4 * c + 4, :]
                return nc.vector.tensor_tensor(rows, psum.rearrange("p (t d) -> p t d", t=4), rows, ALU.add)

            def statistics(c):
                for t in range(4 * c, 4 * c + 4):
                    last = nc.vector.bn_stats(stats[:, t, :], x1[:, t, :])
                return last

            def aggregate(c):
                for t in range(4 * c, 4 * c + 4):
                    last = nc.vector.bn_aggr(mean_var[:, t, :], stats[:, t, :])
                return last

            dve.wait_ge(zeroed, 1)
            for k in range(TILES):
                if k == MAX_AT:
                    take_max(0, 0, MAX_AT % 2, MAX_AT, False)
                entry = k + (k >= MAX_AT)
                pass_a_tile(0, k, entry % 2, entry)
                if k % 16 == 15:
                    split_max(k // 16, 0, entry + 1)
                elif k in (16, 17, 18):
                    split_max(0, k - 15)

            def iteration(i, first, last):
                base, entry = ring_base(i, first), 0
                for s in range(STEPS):
                    for kind, x in ring_step(s, first, last):
                        slot = (base_slot(first) + entry) % 2
                        if kind == "tile":
                            pass_a_tile(i + 1, x, slot, base + entry)
                            if x % 16 < 3:
                                split_max(1 - x // 16, x % 16 + 1)
                        elif kind == "at":
                            dve.wait_ge(a_full, base + entry + 1)
                            nc.vector.tensor_copy(a_t[:, x % 2, :], ring_a[:, slot, 0:512]).then_inc(a_free, 1)
                        elif kind == "pr":
                            dve.wait_ge(res_ready, x + 1)
                            dve.wait_ge(a_full, base + entry + 1)
                            add_rows(x, ring_a[:, slot, 0:512]).then_inc(a_free, 1)
                            dve.wait_ge(a_free, base + entry + 1)
                            link(statistics(x))
                            link(aggregate(x), False)
                        elif kind == "max":
                            take_max(i if x else i + 1, x, slot, base + entry, not (first and x == 1))
                        else:
                            take_out(i - x, x, slot, base + entry)
                        entry += 1
                    if not last and s % NQT == NQT - 1:
                        split_max(s // NQT, 0, base + entry)
                    elif last and s == 0:
                        for step in range(1, 4):
                            split_max(1, step)

            iteration(0, True, False)
            for i in range(1, NG - 1):
                iteration(i, False, False)
            iteration(NG - 1, False, True)

            def inverse_std(n, ts):
                variance(ts)
                newton_step(n, ts)

            def variance(ts):
                nc.vector.tensor_scalar(var_eps[:, ts], mean_var[:, ts, 1], EPS, None, ALU.add).then_inc(var_ready, 1)

            def newton_step(n, ts):
                dve.wait_ge(std_ready, n + 1)
                link(nc.vector.reciprocal(rstd0[:, ts], std[:, ts]))
                link(nc.vector.tensor_tensor(newton[:, ts], rstd0[:, ts], rstd0[:, ts], ALU.mult))
                link(nc.vector.tensor_tensor(newton2[:, ts], newton[:, ts], var_eps[:, ts], ALU.mult))
                link(nc.vector.tensor_scalar(newton[:, ts], newton2[:, ts], -0.5, 1.5, ALU.mult, ALU.add))
                link(nc.vector.tensor_tensor(rstd[:, ts], newton[:, ts], rstd0[:, ts], ALU.mult))
                nc.vector.scalar_tensor_tensor(shift[:, ts], mean_var[:, ts, 0], -1.0, rstd[:, ts], ALU.mult, ALU.mult
                                               ).then_inc(rstd_done, 1)
                dve.wait_ge(rstd_done, n + 1)

            def normalise(c):
                for t in range(4 * c + 2, 4 * c + 4):
                    last = nc.vector.tensor_scalar(x1[:, t, :], x1[:, t, :], mean_var[:, t, 0:1], rstd[:, t:t + 1],
                                                   ALU.subtract, ALU.mult)
                last.then_inc(normed_d, 1)

            def route(c):
                dve.wait_ge(aff_full, c + 1)
                dve.wait_ge(sig_done, c + 1)
                biased = ring_u[:, c % 2, :].rearrange("p (t e) -> p t e", t=4)[:, :, E:2 * E]
                for t in range(4):
                    last = nc.vector.max(top8[:, t, :], biased[:, t, :])
                link(last)
                for t in range(4):
                    last = nc.vector.match_replace(marked[:, t, :], top8[:, t, :], biased[:, t, :], TAKEN)
                last.then_inc(aff_taken, 1)
                dve.wait_ge(aff_taken, c + 1)
                if c >= 2:
                    dve.wait_ge(cw_done, c - 1)
                link(nc.vector.scalar_tensor_tensor(sel_sig[:, c % 2, :, :], marked[:, :, :], TAKEN,
                                                    sig[:, c % 2, :, :], ALU.is_equal, ALU.mult))
                link(nc.vector.tensor_reduce(wsum[:, :], sel_sig[:, c % 2, :, :], AX.X, ALU.add))
                link(nc.vector.tensor_scalar(wsum_eps[:, :], wsum[:, :], 1e-8, None, ALU.add))
                nc.vector.reciprocal(wrec[:, c % 2, :], wsum_eps[:, :]).then_inc(sel_done, 1)

            dve.wait_ge(dve_chain, steps[0])
            dve.wait_ge(st_full, NG * STEPS * HG)
            inverse_std(0, slice(0, NT - 4))
            take_out(NG - 1, 1, (LAST_ENTRY - 1) % 2, LAST_ENTRY - 1)
            dve.wait_ge(a_free, LAST_ENTRY)
            normalise(0)
            for c in range(N_CHUNK + 2):
                if c + 1 < N_CHUNK:
                    normalise(c + 1)
                if c < N_CHUNK:
                    dve.wait_ge(xt_hi, c + 1)
                    nc.vector.tensor_tensor(x_lo[:, 512 * c:512 * c + 512], ring_b[:, c % 2, :],
                                            x_hi[:, 512 * c:512 * c + 512].bitcast(f32), ALU.subtract).then_inc(xt_lo, 1)
                if c == 1:
                    dve.wait_ge(pr_full, 1)
                    add_rows(N_CHUNK - 1, ring_u[:, 1, :]).then_inc(pr_taken, 1)
                    dve.wait_ge(pr_taken, 1)
                    link(statistics(N_CHUNK - 1))
                    link(aggregate(N_CHUNK - 1))
                    inverse_std(1, slice(NT - 4, NT))
                n = c - 2
                if n >= 0:
                    route(n)

            def weigh(unit, cb, q):
                dve.wait_ge(h_act, unit + 1)
                if cb is None:
                    nc.vector.tensor_copy(hid_w[:, q % 2, :], hid[:, q % 2, :]).then_inc(hw_done, 1)
                else:
                    dve.wait_ge(cb_full, cb + 1)
                    nc.vector.tensor_tensor(hid_w[:, q % 2, :], ring_u[:, q % 2, :], hid[:, q % 2, :], ALU.mult
                                            ).then_inc(hw_done, 1)

            def low(unit, q):
                dve.wait_ge(hi_done, unit + 1)
                nc.vector.tensor_tensor(hid_lo[:, q, :], hid_w[:, q % 2, :], hid_hi[:, q, :].bitcast(f32),
                                        ALU.subtract).then_inc(lo_done, 1)

            def units(half, base, cb, n, first, second=False):
                for u in range(n):
                    if half and first:
                        if u < 4:
                            take_sum(u)
                        else:
                            link(statistics(u - 4))
                            link(aggregate(u - 4))
                    if second:
                        if u == 0:
                            variance(slice(0, 16))
                        elif u == 2:
                            newton_step(2, slice(0, 16))
                        elif u >= 4:
                            normalise(u - 4)
                    if not (first and u < 2):
                        dve.wait_ge(lo_done, base + u - 1)
                    weigh(base + u, None if cb is None else cb + u, u % 4)
                    if not (first and u == 0):
                        low(base + u - 1, (u - 1) % 4)

            def take_sum(n):
                dve.wait_ge(yt_full, n + 1)
                add_rows(n, acc[:, n % 4, :]).then_inc(yt_taken, 1)
                dve.wait_ge(yt_taken, n + 1)

            for half in range(2):
                units(half, half * U_HALF, half * 2 * E, 8, True)
                if half:
                    units(half, U_HALF + 8, 2 * E + 8, 8, False, True)
                with dve.Fori(1 + half, E // 4) as j:
                    units(half, half * U_HALF + 8 * j, half * 2 * E + 8 * j, 8, False)
                units(half, half * U_HALF + 2 * E, None, 4, False)
                low((half + 1) * U_HALF - 1, 3)
            for c in range(4, 8):
                take_sum(c)
                link(statistics(c))
                link(aggregate(c))
            inverse_std(3, slice(16, 32))
            for c in range(4, 8):
                normalise(c)

        @block.gpsimd
        def _(pool):
            nc.gpsimd.memset(corr_add[:, :, :], 0.0).then_inc(zeroed, 1)
            nc.gpsimd.memset(v_stage[:, :, :, :], 0.0).then_inc(v_init, 1)
            pool.wait_ge(v_init, 1)
            nc.gpsimd.memset(v_stage[:, :, :, HD:HD + 1], 1.0).then_inc(v_init, 1)
            pool.wait_ge(v_init, 2)

            for j in range(2, 2 * B):
                pool.wait_ge(qk_taken, j + 1)
                if j < 4:
                    pool.wait_ge(low_d, j - 1)
                nc.gpsimd.tensor_tensor(rest[:, j % 2, :], qk32[:, j % 2, :], part_sb[:, j % 3, 0, :],
                                        ALU.subtract).then_inc(rest_p, 1)
                pool.wait_ge(mid, j + 1)
                nc.gpsimd.tensor_tensor(part_sb[:, j % 3, 2, :], rest[:, j % 2, :], part_sb[:, j % 3, 1, :],
                                        ALU.subtract).then_inc(low_p, 1)

            def stage_v(i, part):
                nc.gpsimd.tensor_tensor(
                    v_stage[:, 4 * part:4 * part + 4, :, 0:HD],
                    v_all[:, ds(i, 1), 4 * part:4 * part + 4, :].rearrange("p a t (h c) -> p (a t) h c", h=HG),
                    b_v[:, ds((i % 4) * HG * HD, HG * HD)].rearrange("p (o h c) -> p o h c", o=1, h=HG)
                    .to_broadcast([128, 4, HG, HD]), ALU.add).then_inc(v_staged, 1)

            pool.wait_ge(v_taken, 2 * B)
            pool.wait_ge(ld_const, LD_CONST)
            stage_v(0, 0)
            stage_v(0, 1)
            def iteration(i, first, last):
                for s in range(STEPS):
                    if s == 5 and first:
                        pool.wait_ge(ld_res, 16 * N_CHUNK)
                        for c in range(N_CHUNK):
                            nc.gpsimd.tensor_tensor(
                                x1[:, 4 * c:4 * c + 4, :], x1[:, 4 * c:4 * c + 4, :],
                                b_out[:, :].rearrange("p (o d) -> p o d", o=1).to_broadcast([128, 4, D]),
                                ALU.add).then_inc(res_ready, 1)
                    if s == 2 and not first:
                        pool.wait_ge(pv_done, STEPS * i)
                        stage_v(i, 1)
                    if s == 14 and not last:
                        pool.wait_ge(pv_done, STEPS * i + 12)
                        stage_v(i + 1, 0)
                    d = diag_index(s)
                    if d is not None:
                        kt4 = s % 4
                        pool.wait_ge(exp_done, (STEPS * i + s + 1) * HG)
                        blk = probs[:, s % NP_SLOTS, :, 128 * kt4:128 * kt4 + 128]
                        nc.gpsimd.tensor_tensor(blk, blk, corr_mul[:, ds((i % 4) * HG, HG), :], ALU.mult
                                                ).then_inc(diag_done, 1)

            iteration(0, True, False)
            with pool.Fori(1, NG - 1) as i:
                iteration(i, False, False)
            iteration(NG - 1, False, True)

            pool.wait_ge(a_free, LAST_ENTRY)

            nc.gpsimd.tensor_copy(cent_hi[:, :], cent[:, :]).then_inc(cent_split, 1)
            pool.wait_ge(cent_split, 1)
            nc.gpsimd.tensor_tensor(cent_lo[:, :], cent[:, :], cent_hi[:, :].bitcast(f32), ALU.subtract
                                    ).then_inc(cent_split, 1)
            pool.wait_ge(ws_ld, 16)
            nc.gpsimd.tensor_copy(ws_hi[:, :], ws_raw[:, :]).then_inc(ws_split, 1)
            pool.wait_ge(ws_split, 1)
            nc.gpsimd.tensor_tensor(ws_lo[:, :], ws_raw[:, :], ws_hi[:, :].bitcast(f32), ALU.subtract
                                    ).then_inc(ws_split, 1)
            def split_pair(half, j, par, first):
                n = half * (E // 2) + 2 * j + par
                before = half * U_HALF - 4 if isinstance(j, int) else half * U_HALF + (2 * j + par - 1) * 4
                pool.wait_ge(w_ld[par], (half * (E // 4) + j + 1) * 32)
                for part, (used, done) in enumerate(((h_full, up_split), (dn_done, w_split))):
                    if not first:
                        pool.wait_ge(used, before)
                    cols = slice(128 * part, 128 * part + 128)
                    pool.sem_inc(waited_pool, 1)
                    nc.gpsimd.tensor_copy(w_hi[:, par, cols], w_raw[:, par, cols]).then_inc(w_hi_done, 1)
                    pool.wait_ge(w_hi_done, 2 * n + part + 1)
                    nc.gpsimd.tensor_tensor(w_lo[:, par, cols], w_raw[:, par, cols], w_hi[:, par, cols].bitcast(f32),
                                            ALU.subtract).then_inc(done, 1)

            for par in range(2):
                split_pair(0, 0, par, True)

            for c in range(N_CHUNK):
                pool.wait_ge(sel_done, c + 1)
                nc.gpsimd.tensor_tensor(cw[:, c % 2, :, :], sel_sig[:, c % 2, :, :],
                                        wrec[:, c % 2, :].rearrange("p (t o) -> p t o", o=1).to_broadcast([128, 4, E]),
                                        ALU.mult).then_inc(cw_done, 1)
                pool.wait_ge(cw_done, c + 1)
                pool.wait_ge(cw_hi_done, c + 1)
                nc.gpsimd.tensor_tensor(cw_rest[:, c % 2, :, :], cw[:, c % 2, :, :], cw_half[:, c % 2, :, 0:E],
                                        ALU.subtract).then_inc(pool_chain, 1)
                pool.wait_ge(pool_chain, c + 1)
                nc.gpsimd.tensor_scalar(cw_half[:, c % 2, :, E:2 * E], cw_rest[:, c % 2, :, :], 4096.0, None, ALU.mult
                                        ).then_inc(cw_split, 1)

            for half in range(2):
                if half:
                    for par in range(2):
                        split_pair(half, 0, par, False)
                with pool.Fori(1, E // 4) as j:
                    for par in range(2):
                        split_pair(half, j, par, False)


def kernel(L0_attn_x, L0_attn_W_qkv, L0_attn_b_qkv, L0_attn_W_out, L0_attn_b_out, L0_ffn_centroids,
           L0_ffn_expert_biases, L0_ffn_Ws_up, L0_ffn_Ws_down, L0_ffn_W_up, L0_ffn_W_down):
    import concourse.bacc as bacc
    from concourse.bass_utils import run_bass_kernel_spmd

    x = np.asarray(L0_attn_x).reshape(T, D)
    row = np.arange(D).reshape(H // HG, HG, HD).transpose(0, 2, 1).ravel()
    row = np.concatenate([row, D + row, 2 * D + np.arange(D)])
    w_qkv, b_qkv = np.asarray(L0_attn_W_qkv)[row], np.asarray(L0_attn_b_qkv)[row]
    pairs = np.concatenate([
        np.asarray(L0_ffn_W_up).reshape(E // 2, 2, D, F).transpose(0, 2, 1, 3).reshape(E // 2, D, 2 * F),
        np.asarray(L0_ffn_W_down).reshape(E // 2, 2 * F, D)], axis=2)
    shared = np.zeros((D, 2 * F + D), np.float32)
    shared[:, 0:F] = np.asarray(L0_ffn_Ws_up)
    shared[0:F, 2 * F:] = np.asarray(L0_ffn_Ws_down)
    host = {
        "x": x, "x_t": x.T, "w_qkv_t": w_qkv.T,
        "b_qk": b_qkv[0:2 * D].reshape(2, D).T, "b_v": b_qkv[2 * D:].reshape(1, D),
        "w_out_t": np.asarray(L0_attn_W_out).T, "b_out": np.asarray(L0_attn_b_out).reshape(1, D),
        "cent_t": np.tile(np.asarray(L0_ffn_centroids).T, 2),
        "e_bias": np.pad(np.asarray(L0_ffn_expert_biases).reshape(E, 1), ((E, 0), (0, 0))),
        "w_shared": shared, "w_pairs": pairs,
        **host_constants(),
    }
    nc = bacc.Bacc("TRN2", target_bir_lowering=False, num_devices=1)
    nc.disable_value_cache = True
    arrays, aps = {}, {}
    for name, v in host.items():
        v = np.ascontiguousarray(v)
        arrays["in_" + name] = v
        aps[name] = nc.dram_tensor("in_" + name, v.shape, mybir.dt.from_np(v.dtype), kind="ExternalInput").ap()
    out = nc.dram_tensor("out_0", [T, D], mybir.dt.float32, kind="ExternalOutput").ap()
    build(nc, aps, out)
    r = run_bass_kernel_spmd(nc, [arrays], core_ids=[0])
    return r.results[0]["out_0"].reshape(B, S, D)
```
